# Optimizing a Trainium2 kernel written in Bass

```python
import numpy as np
import jax
import jax.numpy as jnp

def _softmax(x, axis=-1):
    return jax.nn.softmax(x, axis=axis)

def _gelu(x):
    return jax.nn.gelu(x, approximate=True)

def _silu(x):
    return jax.nn.silu(x)

def _sigmoid(x):
    return jax.nn.sigmoid(x)

def _layernorm(x, axis=-1, eps=1e-05):
    m = jnp.mean(x, axis=axis, keepdims=True)
    v = jnp.var(x, axis=axis, keepdims=True)
    return (x - m) / jnp.sqrt(v + eps)

def _scatter_add(tgt, idx, src, axis=0):
    return tgt.at[idx].add(src)

def _segment_sum(src, seg, n):
    return jax.ops.segment_sum(src, seg, n)
kernel_name = 'mk_adaln_ffn_d2_seqx_r8_b57a33'

def setup_inputs(seed: int=0):
    np.random.seed(seed)
    _w = jnp.asarray

    def _rec_inputs():
        import jax
        import jax.numpy as jnp
        _rk = jax.random.key(seed)
        x = -0.000125 + 0.9999 * jax.random.normal(jax.random.fold_in(_rk, 1), (128, 32, 512), jnp.float32)
        _lenS = 32 - jax.random.randint(jax.random.fold_in(_rk, 7), (128,), 0, max(1, 32 // 4) + 1, jnp.int32)
        _lenS2 = 32 - jax.random.randint(jax.random.fold_in(_rk, 8), (128,), 0, max(1, 32 // 4) + 1, jnp.int32)
        cond_128 = 0.0061147 + 1.02565 * jax.random.normal(jax.random.fold_in(_rk, 11), (128, 128), jnp.float32)
        fside_S_0 = -0.022604 + 0.987366 * jax.random.normal(jax.random.fold_in(_rk, 12), (32,), jnp.float32)
        return (x, cond_128, fside_S_0)
    x, cond_128, fside_S_0 = _rec_inputs()

    def _L0_cond_setup():
        import jax, jax.numpy as jnp
        import numpy as np
        from jax import lax
        N, C_IN, L = (32, 32, 512)
        C_OUT, K, GROUPS = (32, 9, 4)
        C_DIM, PAD, STRIDE = (128, 4, 1)
        key = jax.random.key(seed)
        k1, k2, k3, k4, k5 = jax.random.split(key, 5)
        x = jax.random.normal(k1, (N, C_IN, L), dtype=jnp.float32)
        c = jax.random.normal(k2, (N, C_DIM), dtype=jnp.float32)
        weight = jax.random.normal(k3, (C_OUT, C_IN // GROUPS, K), dtype=jnp.float32)
        c_weight = jax.random.normal(k4, (C_OUT, C_DIM), dtype=jnp.float32)
        bias = jax.random.normal(k5, (C_OUT,), dtype=jnp.float32)
        return {'x': x, 'c': c, 'weight': weight, 'c_weight': c_weight, 'bias': bias}
    _L0_cond_all = _L0_cond_setup()
    _L0_cond_in = {k: v for k, v in _L0_cond_all.items() if k in ('weight', 'c_weight')}
    del _L0_cond_all

    def _L0_ffn_setup():
        import jax, jax.numpy as jnp
        import numpy as np
        TOP_K = 2
        key = jax.random.key(seed)
        k0, k1, k2 = jax.random.split(key, 3)
        B, S, D, H, E = (4, 256, 512, 512, 8)
        sc = 1.0 / np.sqrt(D).astype(np.float32)
        x = jax.random.normal(k0, (B, S, D), dtype=jnp.float32)
        W_gate = jax.random.normal(k1, (D, E), dtype=jnp.float32) * sc
        b_gate = jnp.zeros((E,), dtype=jnp.float32)
        W_e = jax.random.normal(k2, (E, D, H), dtype=jnp.float32) * sc
        b_e = jnp.zeros((E, H), dtype=jnp.float32)
        return {'x': x, 'W_gate': W_gate, 'b_gate': b_gate, 'W_e': W_e, 'b_e': b_e}
    _L0_ffn_all = _L0_ffn_setup()
    _L0_ffn_in = {k: v for k, v in _L0_ffn_all.items() if k in ('W_gate', 'b_gate', 'W_e', 'b_e')}
    del _L0_ffn_all

    def _L1_cond_setup():
        import jax, jax.numpy as jnp
        import numpy as np
        K = 8
        T = 1.0
        D_EMBD = 128
        IN_C = 32
        OUT_C = 32
        BS = 32
        H = 512
        HID = 128
        key = jax.random.key(seed)
        ks = jax.random.split(key, 10)
        s = lambda fan_in: 1.0 / np.sqrt(fan_in)
        return {'x': jax.random.normal(ks[0], (BS, IN_C, H), dtype=jnp.float32), 'embedding': jax.random.normal(ks[1], (BS, D_EMBD), dtype=jnp.float32), 'W0': jax.random.normal(ks[2], (D_EMBD, HID), dtype=jnp.float32) * s(D_EMBD), 'b0': jnp.zeros((HID,), dtype=jnp.float32), 'W1': jax.random.normal(ks[3], (HID, HID), dtype=jnp.float32) * s(HID), 'b1': jnp.zeros((HID,), dtype=jnp.float32), 'W2': jax.random.normal(ks[4], (HID, K), dtype=jnp.float32) * s(HID), 'b2': jnp.zeros((K,), dtype=jnp.float32), 'weight': jax.random.normal(ks[5], (K, OUT_C, IN_C, 1), dtype=jnp.float32) * s(IN_C), 'bias_k': jax.random.normal(ks[6], (K, OUT_C), dtype=jnp.float32) * 0.1}
    _L1_cond_all = _L1_cond_setup()
    _L1_cond_in = {k: v for k, v in _L1_cond_all.items() if k in ('W0', 'b0', 'W1', 'b1', 'W2', 'b2', 'weight', 'bias_k')}
    del _L1_cond_all

    def _L1_ffn_setup():
        import jax, jax.numpy as jnp
        import numpy as np
        B, S, IN, OUT = (4, 256, 512, 512)
        PACK = 8

        def _dequant(qweight, scales, zeros):
            qw = jax.lax.bitcast_convert_type(qweight, jnp.uint32)
            shifts = jnp.arange(PACK, dtype=jnp.uint32) * jnp.uint32(4)
            nib = qw[:, None, :] >> shifts[None, :, None] & jnp.uint32(15)
            q = nib.reshape(-1, qw.shape[1]).astype(jnp.float32)
            return scales[:, 0][None, :] * q - zeros[:, 0][None, :]
        key = jax.random.key(seed)
        k1, k2, k3, k4, k5 = jax.random.split(key, 5)
        x = jax.random.normal(k1, (B, S, IN), dtype=jnp.float32)
        qweight = jax.random.randint(k2, (IN // PACK, OUT), 0, 2147483647, dtype=jnp.int32)
        scales = jax.random.uniform(k3, (OUT, 1), dtype=jnp.float32, minval=0.005, maxval=0.02)
        zeros = jax.random.uniform(k4, (OUT, 1), dtype=jnp.float32, minval=0.0, maxval=0.15)
        bias = jax.random.normal(k5, (OUT,), dtype=jnp.float32) * 0.02
        return {'x': x, 'qweight': qweight, 'scales': scales, 'zeros': zeros, 'bias': bias}
    _L1_ffn_all = _L1_ffn_setup()
    _L1_ffn_in = {k: v for k, v in _L1_ffn_all.items() if k in ('qweight', 'scales', 'zeros', 'bias')}
    del _L1_ffn_all
    return {'x': x, 'cond_128': cond_128, 'fside_S_0': fside_S_0, 'L0_cond_weight': _L0_cond_in['weight'], 'L0_cond_c_weight': _L0_cond_in['c_weight'], 'L0_ffn_W_gate': _L0_ffn_in['W_gate'], 'L0_ffn_b_gate': _L0_ffn_in['b_gate'], 'L0_ffn_W_e': _L0_ffn_in['W_e'], 'L0_ffn_b_e': _L0_ffn_in['b_e'], 'L1_cond_W0': _L1_cond_in['W0'], 'L1_cond_b0': _L1_cond_in['b0'], 'L1_cond_W1': _L1_cond_in['W1'], 'L1_cond_b1': _L1_cond_in['b1'], 'L1_cond_W2': _L1_cond_in['W2'], 'L1_cond_b2': _L1_cond_in['b2'], 'L1_cond_weight': _L1_cond_in['weight'], 'L1_cond_bias_k': _L1_cond_in['bias_k'], 'L1_ffn_qweight': _L1_ffn_in['qweight'], 'L1_ffn_scales': _L1_ffn_in['scales'], 'L1_ffn_zeros': _L1_ffn_in['zeros'], 'L1_ffn_bias': _L1_ffn_in['bias']}

def reference(x, cond_128, fside_S_0, L0_cond_weight, L0_cond_c_weight, L0_ffn_W_gate, L0_ffn_b_gate, L0_ffn_W_e, L0_ffn_b_e, L1_cond_W0, L1_cond_b0, L1_cond_W1, L1_cond_b1, L1_cond_W2, L1_cond_b2, L1_cond_weight, L1_cond_bias_k, L1_ffn_qweight, L1_ffn_scales, L1_ffn_zeros, L1_ffn_bias):
    import jax
    import jax.numpy as jnp

    def _L0_cond_ref(x, c, weight, c_weight, bias):
        import jax, jax.numpy as jnp
        import numpy as np
        from jax import lax
        N, C_IN, L = (32, 32, 512)
        C_OUT, K, GROUPS = (32, 9, 4)
        C_DIM, PAD, STRIDE = (128, 4, 1)
        out = lax.conv_general_dilated(x, weight, window_strides=(STRIDE,), padding=[(PAD, PAD)], dimension_numbers=('NCH', 'OIH', 'NCH'), feature_group_count=GROUPS)
        ctx = jnp.einsum('nd,od->no', c, c_weight)
        out = out + ctx[:, :, None] + bias[None, :, None]
        return out

    def _L0_ffn_ref(x, W_gate, b_gate, W_e, b_e):
        import jax, jax.numpy as jnp
        import numpy as np
        TOP_K = 2
        logits = x @ W_gate + b_gate
        _, top_idx = jax.lax.top_k(logits, TOP_K)
        y_all = jax.nn.relu(jnp.einsum('bsd,edh->bseh', x, W_e) + b_e)
        y = jnp.take_along_axis(y_all, top_idx[..., None], axis=2)
        return y.mean(axis=2)

    def _L1_cond_ref(x, embedding, W0, b0, W1, b1, W2, b2, weight, bias_k):
        import jax, jax.numpy as jnp
        import numpy as np
        K = 8
        T = 1.0
        D_EMBD = 128
        IN_C = 32
        OUT_C = 32
        BS = 32
        H = 512
        HID = 128
        h = jax.nn.gelu(embedding @ W0 + b0, approximate=False)
        h = jax.nn.gelu(h @ W1 + b1, approximate=False)
        att = jax.nn.softmax((h @ W2 + b2) / T, axis=-1)
        agg_w = jnp.einsum('bk,koi->boi', att, weight[..., 0])
        agg_b = att @ bias_k
        out = jnp.einsum('boi,bih->boh', agg_w, x) + agg_b[:, :, None]
        return out

    def _L1_ffn_ref(x, qweight, scales, zeros, bias):
        import jax, jax.numpy as jnp
        import numpy as np
        B, S, IN, OUT = (4, 256, 512, 512)
        PACK = 8

        def _dequant(qweight, scales, zeros):
            qw = jax.lax.bitcast_convert_type(qweight, jnp.uint32)
            shifts = jnp.arange(PACK, dtype=jnp.uint32) * jnp.uint32(4)
            nib = qw[:, None, :] >> shifts[None, :, None] & jnp.uint32(15)
            q = nib.reshape(-1, qw.shape[1]).astype(jnp.float32)
            return scales[:, 0][None, :] * q - zeros[:, 0][None, :]
        W = _dequant(qweight, scales, zeros)
        out = jnp.einsum('bsi,io->bso', x, W) + bias
        return out
    x = x + _L0_ffn_ref(_L0_cond_ref(x, cond_128, L0_cond_weight, L0_cond_c_weight, fside_S_0), L0_ffn_W_gate, L0_ffn_b_gate, L0_ffn_W_e, L0_ffn_b_e)
    x = x + _L1_ffn_ref(_L1_cond_ref(x, cond_128, L1_cond_W0, L1_cond_b0, L1_cond_W1, L1_cond_b1, L1_cond_W2, L1_cond_b2, L1_cond_weight, L1_cond_bias_k), L1_ffn_qweight, L1_ffn_scales, L1_ffn_zeros, L1_ffn_bias)
    return x

_drawn_inputs = setup_inputs


def setup_inputs(seed=0):
    import zlib

    import numpy as np

    out = dict(_drawn_inputs(seed))
    spreads = {'L0_ffn_b_gate': (0.0, 2.0),
     'L0_ffn_b_e': (0.0, 2.0),
     'L1_cond_b0': (0.0, 0.1),
     'L1_cond_b1': (0.0, 0.1),
     'L1_cond_b2': (0.0, 0.1)}
    factors = {'L1_cond_bias_k': 2.823, 'L1_ffn_bias': 64.0}
    for name, (base, spread) in spreads.items():
        noise = np.random.default_rng([zlib.crc32(name.encode()), seed]).standard_normal(out[name].shape)
        drawn = base * np.exp(spread * noise) if base else spread * noise
        out[name] = jnp.asarray(drawn.astype(out[name].dtype))
    for name, factor in factors.items():
        out[name] = (out[name] * factor).astype(out[name].dtype)
    return out
```

```python
from contextlib import ExitStack

import numpy as np

import concourse.bass as bass
from concourse import mybir

F32 = mybir.dt.float32
BF16 = mybir.dt.bfloat16
I32 = mybir.dt.int32
U32 = mybir.dt.uint32
ALU = mybir.AluOpType
ACT = mybir.ActivationFunctionType
AX = mybir.AxisListType

P = 128
N, C, L = 128, 32, 512
SUB = P // C
NG = N // SUB
TAPS, PAD, CG = 9, 4, 8
PH = L // P
SHIFTS = 3
KW = TAPS + 2 * (PH - 1)
E = 8
REGION = N * C + P
NT = (2 * N * C - E) // P + E
U = 4
XR = 4


def live(i, n):
    return not isinstance(i, int) or 0 <= i < n


def wait(eng, sem, value):
    if not isinstance(value, int) or value > 0:
        eng.wait_ge(sem, value)


def stepped(eng, step, first, lo, hi, last):
    assert (hi - lo) % U == 0 and lo % U == 0
    for i in range(first, lo):
        step(i, i % U)
    with eng.Fori(0, (hi - lo) // U) as k:
        base = k * U + lo
        for j in range(U):
            step(base + j, j)
    for i in range(hi, last):
        step(i, i % U)


def ring_count(i, j, ring):
    return (i - j % ring) * (16 // ring) + 16


def build_program(nc, x, cond, fside, conv_w, ctx_w, w_gate, b_gate, w_e, b_e,
                  w0, b0, w1, b1, w2, b2, mix_w, mix_b, qweight, scales, zeros, bias, out):
    ctx = ExitStack()
    with ctx:
        def sb(name, shape, dt=F32):
            return ctx.enter_context(nc.sbuf_tensor(name, shape, dt))

        def sem(name):
            return ctx.enter_context(nc.semaphore(name))

        def dram(name, shape):
            return nc.dram_tensor(name, shape, F32, kind="Internal").ap()

        lists_d = dram("lists_d", (E * REGION, L))
        result_d = dram("result_d", (NT * P, L))
        ctx_d = dram("ctx_d", (N, C))
        mixb_d = dram("mixb_d", (N, C))
        mix_d = dram("mix_d", (N, C, C))

        x_g = x.rearrange("(g s) c l -> g (s c) l", s=SUB)
        out_g = out.rearrange("(g s) c l -> g (s c) l", s=SUB)

        we = sb("we", [P, E, PH, L])
        be_bc = sb("be_bc", [P, E, L])
        ctx_bc = sb("ctx_bc", [P, N * C])
        mixb_bc = sb("mixb_bc", [P, N * C])
        mix_bd = sb("mix_bd", [P, NG, P])
        wq = sb("wq", [P, 4, L])
        scale_bc = sb("scale_bc", [P, L])
        zero_bc = sb("zero_bc", [P, L])
        bias_bc = sb("bias_bc", [P, L])
        xt = sb("xt", [P, XR, L])
        ring_a = sb("ring_a", [P, 2, L])
        phases = sb("phases", [P, 2, SUB, P + 2])
        hT = sb("hT", [P, 2, L])
        htok = sb("htok", [P, U, L])
        ring_b = sb("ring_b", [P, 2, L])
        orow = sb("orow", [P, 2, L])
        ident = sb("ident", [P, P])
        before = sb("before", [P, P], BF16)
        ones = sb("ones", [P, P], BF16)
        wconv = sb("wconv", [P, SHIFTS, PH, C])
        wfull = sb("wfull", [C, C, KW])
        wg = sb("wg", [P, PH, P])
        bg_bc = sb("bg_bc", [P, E])
        iota_e = sb("iota_e", [P, E])
        region = sb("region", [P, E])
        lane = sb("lane", [P, 1])
        base = sb("base", [P, E])
        logit = sb("logit", [P, E])
        top = sb("top", [P, E])
        topi = sb("topi", [P, E], U32)
        chosen1 = sb("chosen1", [P, E])
        chosen = sb("chosen", [P, U, E], BF16)
        rank = sb("rank", [P, E])
        picked = sb("picked", [P, 2, E])
        expert_of = sb("expert_of", [P, NG, 2])
        row_of = sb("row_of", [P, NG, 2])
        row_i = sb("row_i", [P, U, 2], I32)
        tcount = sb("tcount", [P, E])
        tint = sb("tint", [P, E], I32)
        tshift = sb("tshift", [P, E], I32)
        prefix = sb("prefix", [P, 4, 2 * E])
        tstart = sb("tstart", [P, E])
        offs = sb("offs", [P, E])
        doffs = sb("doffs", [P, E])
        mask = sb("mask", [P, E])
        mprod = sb("mprod", [P, E])
        tsum = sb("tsum", [P, 4])
        used = sb("used", [P, 1])
        tab_f = sb("tab_f", [P, 2])
        tab = sb("tab", [2, P], I32)
        tail_i = sb("tail_i", [1, E], I32)
        shift_e = sb("shift_e", [P, NG * 2])
        shift_s = sb("shift_s", [P, NG * 2])
        place_i = sb("place_i", [P, NG, 2], I32)
        gidx = sb("gidx", [P, 2, 2], I32)
        cond_sb = sb("cond_sb", [N, P])
        condT = sb("condT", [P, N])
        cw_sb = sb("cw_sb", [C, P])
        cwT = sb("cwT", [P, C])
        fs_bc = sb("fs_bc", [P, C])
        ctx_sb = sb("ctx_sb", [N, C])
        w0_sb = sb("w0_sb", [P, P])
        w1_sb = sb("w1_sb", [P, P])
        w2_sb = sb("w2_sb", [P, E])
        b0_sb = sb("b0_sb", [P, 1])
        b1_sb = sb("b1_sb", [P, 1])
        b2_bc = sb("b2_bc", [P, E])
        mixb_w = sb("mixb_w", [E, C])
        g0 = sb("g0", [P, N])
        g1 = sb("g1", [P, N])
        att = sb("att", [N, E])
        att_m = sb("att_m", [N, 1])
        att_x = sb("att_x", [N, E])
        att_s = sb("att_s", [N, 1])
        att_r = sb("att_r", [N, 1])
        att_n = sb("att_n", [N, E])
        attT = sb("attT", [E, N])
        mixb_sb = sb("mixb_sb", [N, C])
        mixw_sb = ring_b[0:E, :, :].rearrange("k h n -> k (h n)")
        mix_sb = sb("mix_sb", [N, C, C])
        wsel = htok[0:C, 1:4, :].rearrange("o a (b q i) -> o (a b) q i", q=PH, i=C)
        lane_i = sb("lane_i", [P, 1], I32)
        odd_i = sb("odd_i", [P, 1], I32)
        odd = sb("odd", [P, 1])
        even = sb("even", [P, 1])

        bank = [ctx.enter_context(nc.psum_tensor(f"bank{i}", [P, 512], F32)) for i in range(8)]
        ps_xT, ps_ph, ps_conv, ps_tok, ps_gate, ps_rank, ps_misc = (
            bank[0], bank[1], bank[2:4], bank[4], bank[5], bank[6], bank[7])
        ps_lT, ps_exp = bank[0:2], bank[2:4]
        ps_mix, ps_lin = bank[4:6], bank[2:4]

        consts = sem("consts")
        convw_in = sem("convw_in")
        cond_in = sem("cond_in")
        gate_in = sem("gate_in")
        bg_in = sem("bg_in")
        mlp_in = sem("mlp_in")
        q_in = sem("q_in")
        be_in = sem("be_in")
        we_in = sem("we_in")
        x_in = [sem(f"x_in{i}") for i in range(XR)]
        wsel_ready = sem("wsel_ready")
        wT_done = sem("wT_done")
        wconv_ready = sem("wconv_ready")
        condT_done = sem("condT_done")
        condT_ready = sem("condT_ready")
        ctx_mm = sem("ctx_mm")
        ctx_ready = sem("ctx_ready")
        ctx_out = sem("ctx_out")
        ctx_in = sem("ctx_in")
        deq = sem("deq")
        xT_done = sem("xT_done")
        xT_ready = sem("xT_ready")
        ph_done = sem("ph_done")
        ph_ready = sem("ph_ready")
        conv_done = sem("conv_done")
        hT_ready = sem("hT_ready")
        gate_done = sem("gate_done")
        tok_done = sem("tok_done")
        tok_ready = sem("tok_ready")
        logit_ready = sem("logit_ready")
        top_ready = sem("top_ready")
        topi_ready = sem("topi_ready")
        expert_ready = sem("expert_ready")
        chosen1_ready = sem("chosen1_ready")
        chosen_ready = sem("chosen_ready")
        rank_done = sem("rank_done")
        rank_ready = sem("rank_ready")
        base_ready = sem("base_ready")
        row_ready = sem("row_ready")
        rowi_ready = sem("rowi_ready")
        scatter_go = sem("scatter_go")
        scattered = [sem(f"scattered{i}") for i in range(U)]
        table = sem("table")
        tab_done = sem("tab_done")
        tab_ready = sem("tab_ready")
        tail_out = sem("tail_out")
        place_ready = sem("place_ready")
        mlp_mm = sem("mlp_mm")
        mlp_ev = sem("mlp_ev")
        mix_out = sem("mix_out")
        mix_in = sem("mix_in")
        list_in = [sem(f"list_in{i}") for i in range(U)]
        lT_done = sem("lT_done")
        lT_ready = sem("lT_ready")
        exp_done = sem("exp_done")
        sum_ready = sem("sum_ready")
        result_ready = sem("result_ready")
        result_out = [sem(f"result_out{i}") for i in range(2)]
        gidx_ready = sem("gidx_ready")
        gather_go = sem("gather_go")
        gathered = [sem(f"gathered{i}") for i in range(2)]
        x3_in = [sem(f"x3_in{i}") for i in range(XR)]
        ya_ready = sem("ya_ready")
        y_ready = sem("y_ready")
        mixed_done = sem("mixed_done")
        mixed_ready = sem("mixed_ready")
        yb_ready = sem("yb_ready")
        lin_done = sem("lin_done")
        out_ready = sem("out_ready")
        out_out = [sem(f"out_out{i}") for i in range(2)]

        N_CONSTS = 16
        N_DEQ = 7 + 4 * 4
        zeros_t = orow[:, 0, :]
        lo1, hi1 = U, NG - U
        lo2, hi2 = U, (NT - 1) // U * U

        block = ctx.enter_context(nc.Block())

        @block.sync
        def _(sp):
            for g in range(2):
                sp.dma_start(xt[:, g, :], x_g[g]).then_inc(x_in[g], 16)
            sp.dma_start(cond_sb[:, :], cond).then_inc(cond_in, 16)
            sp.dma_start(cw_sb[:, :], ctx_w).then_inc(cond_in, 16)
            sp.dma_start(fs_bc[:, :], fside.rearrange("(a c) -> a c", a=1).to_broadcast((P, C))).then_inc(cond_in, 16)
            for g in range(2, XR):
                sp.dma_start(xt[:, g, :], x_g[g]).then_inc(x_in[g], 16)
            sp.wait_ge(ctx_ready, 1)
            sp.dma_start(ctx_d, ctx_sb[:, :]).then_inc(ctx_out, 16)
            sp.wait_ge(ctx_out, 16)
            sp.dma_start(ctx_bc[:, :], ctx_d.rearrange("(a n) c -> a (n c)", a=1).to_broadcast((P, N * C))).then_inc(ctx_in, 16)

            def load_we(e):
                return sp.dma_start(we[:, bass.ds(e, 1), :, :].rearrange("m a p n -> m (a p n)"),
                                    w_e[bass.ds(e, 1)].rearrange("a (m p) n -> m (a p n)", p=PH)).then_inc(we_in, 16)

            load_we(0)
            with sp.Fori(0, NG // XR - 1) as k:
                for j in range(XR):
                    sp.wait_ge(xT_done, k * XR + j + 1)
                    sp.dma_start(xt[:, j, :], x_g[bass.ds(k * XR + XR + j, 1)].rearrange("a p l -> p (a l)")).then_inc(x_in[j], 16)
                load_we(k + 1)

            for s in scattered:
                sp.wait_ge(s, 32 * (NG // U))
            sp.wait_ge(tab_ready, 2)
            for e in range(E):
                end = sp.value_load(tail_i[0:1, e:e + 1], min_val=e * REGION, max_val=(e + 1) * REGION - P)
                sp.dma_start(lists_d[bass.ds(end, P), :], zeros_t).then_inc(tail_out, 16)
            sp.wait_ge(tail_out, 16 * E)

            def list_step(s, j):
                a = s + 3
                if live(a, NT):
                    ja = (j + 3) % U
                    row = sp.value_load(tab[0:1, bass.ds(a, 1)], min_val=0, max_val=E * REGION - P)
                    wait(sp, lT_done, a - 3)
                    sp.dma_start(htok[:, ja, :], lists_d[bass.ds(row, P), :]).then_inc(list_in[ja], 16)
                if live(s, NT):
                    wait(sp, result_ready, s + 1)
                    sp.dma_start(result_d[bass.ds(s * P, P), :], ring_b[:, j % 2, :]).then_inc(result_out[j % 2], 16)

            stepped(sp, list_step, -3, lo2, hi2 - U, NT)

            def row_step(g, j):
                a = g + 3
                if live(a, NG):
                    ja = (j + 3) % U
                    wait(sp, ya_ready, a - 3)
                    sp.dma_start(xt[:, ja, :], x_g[bass.ds(a, 1)].rearrange("a p l -> p (a l)")).then_inc(x3_in[ja], 16)
                if live(g, NG):
                    wait(sp, out_ready, g + 1)
                    sp.dma_start(out_g[bass.ds(g, 1)].rearrange("a p l -> p (a l)"), orow[:, j % 2, :]).then_inc(out_out[j % 2], 16)

            stepped(sp, row_step, -3, lo1, hi1, NG)
            for s in out_out:
                sp.wait_ge(s, 16 * (NG // 2))

        @block.gpsimd
        def _(pool):
            pool.memset(ident[:, :], 0.0).then_inc(consts, 1)
            pool.memset(wfull[:, :, :], 0.0).then_inc(consts, 1)
            pool.memset(phases[:, :, :, :], 0.0).then_inc(consts, 1)
            pool.memset(wg[:, :, :], 0.0).then_inc(consts, 1)
            pool.wait_ge(consts, 4)
            pool.affine_select(out=ident[:, :], in_=ident[:, :], compare_op=ALU.not_equal, fill=1.0, base=0,
                               pattern=[[-1, P]], channel_multiplier=1).then_inc(consts, 1)
            for s in range(C // CG):
                rows = slice(s * CG, (s + 1) * CG)
                pool.dma_start(wfull[rows, rows, PH - 1:PH - 1 + TAPS], conv_w[rows]).then_inc(convw_in, 16)
            pool.dma_start(wg[:, :, 0:E], w_gate.rearrange("(m p) e -> m p e", p=PH)).then_inc(gate_in, 16)
            pool.memset(ones[:, :], 1.0).then_inc(consts, 1)
            pool.memset(before[:, :], 1.0).then_inc(consts, 1)
            pool.iota(iota_e[:, :], pattern=[[1, E]], base=0, channel_multiplier=0, allow_small_or_imprecise_dtypes=True).then_inc(consts, 1)
            pool.iota(region[:, :], pattern=[[REGION, E]], base=0, channel_multiplier=0, allow_small_or_imprecise_dtypes=True).then_inc(consts, 1)
            pool.iota(lane[:, :], pattern=[[0, 1]], base=0, channel_multiplier=1, allow_small_or_imprecise_dtypes=True).then_inc(consts, 1)
            pool.iota(base[:, :], pattern=[[REGION, E]], base=0, channel_multiplier=0, allow_small_or_imprecise_dtypes=True).then_inc(consts, 1)
            pool.wait_ge(consts, 7)
            pool.affine_select(out=before[:, :], in_=before[:, :], compare_op=ALU.is_ge, fill=0.0, base=-1,
                               pattern=[[1, P]], channel_multiplier=-1).then_inc(consts, 1)
            pool.memset(prefix[:, :, :], 0.0).then_inc(consts, 1)
            pool.memset(zeros_t, 0.0).then_inc(consts, 1)
            pool.iota(lane_i[:, :], pattern=[[0, 1]], base=0, channel_multiplier=1).then_inc(consts, 1)
            pool.memset(mix_bd[:, :, :], 0.0).then_inc(consts, 1)

            def scatter_step(g, j):
                wait(pool, tok_ready, g + 1)
                wait(pool, rowi_ready, g + 1)
                pool.sem_inc(scatter_go, 1)
                for k in range(2):
                    pool.indirect_dma_start(lists_d, bass.IndirectOffsetOnAxis(ap=row_i[:, j, k:k + 1], axis=0),
                                            htok[:, j, :], None, bounds_check=E * REGION - 1,
                                            oob_is_err=False).then_inc(scattered[j], 16)

            stepped(pool, scatter_step, 0, lo1, hi1, NG)

            for i, s in enumerate(result_out):
                pool.wait_ge(s, 16 * ((NT + 1 - i) // 2))
            pool.wait_ge(place_ready, 1)

            def gather(g, j):
                wait(pool, gathered[j % 2], (g - j % 2) * 16)
                wait(pool, y_ready, g - 1)
                pool.sem_inc(gather_go, 1)
                pool.tensor_copy(gidx[:, j % 2, :], place_i[:, bass.ds(g, 1), :].rearrange("p a k -> p (a k)")).then_inc(gidx_ready, 1)
                wait(pool, gidx_ready, g + 1)
                pool.sem_inc(gather_go, 1)
                for k in range(2):
                    pool.indirect_dma_start(htok[:, 2 * (j % 2) + k, :], None, result_d,
                                            bass.IndirectOffsetOnAxis(ap=gidx[:, j % 2, k:k + 1], axis=0),
                                            bounds_check=NT * P - 1, oob_is_err=False).then_inc(gathered[j % 2], 16)

            def bias_add(g, j):
                wait(pool, y_ready, g + 1)
                wait(pool, out_ready, g - 1)
                pool.tensor_tensor(ring_b[:, j % 2, :], ring_a[:, j % 2, :], bias_bc[:, :], ALU.add).then_inc(yb_ready, 1)

            def step3(g, j):
                if live(g + 2, NG):
                    gather(g + 2, (j + 2) % U)
                if live(g, NG):
                    bias_add(g, j)

            stepped(pool, step3, -2, lo1, hi1, NG)

        @block.scalar
        def _(act):
            act.dma_start(bg_bc[:, :], b_gate.rearrange("(a e) -> a e", a=1).to_broadcast((P, E))).then_inc(bg_in, 16)
            for u in range(2):
                act.dma_start(htok[u:P:2, 0, :].bitcast(I32), qweight).then_inc(q_in, 16)
            act.dma_start(scale_bc[:, :], scales.rearrange("n a -> a n").to_broadcast((P, L))).then_inc(q_in, 16)
            act.dma_start(zero_bc[:, :], zeros.rearrange("n a -> a n").to_broadcast((P, L))).then_inc(q_in, 16)
            act.dma_start(bias_bc[:, :], bias.rearrange("(a n) -> a n", a=1).to_broadcast((P, L))).then_inc(q_in, 16)
            for dst, src in ((w0_sb[:, :], w0), (w1_sb[:, :], w1), (w2_sb[:, :], w2),
                             (b0_sb[:, :], b0.rearrange("(n a) -> n a", a=1)),
                             (b1_sb[:, :], b1.rearrange("(n a) -> n a", a=1)),
                             (b2_bc[:, :], b2.rearrange("(a e) -> a e", a=1).to_broadcast((P, E))),
                             (mixw_sb, mix_w.rearrange("k o i a -> k (o i a)")),
                             (mixb_w[:, :], mix_b)):
                act.dma_start(dst, src).then_inc(mlp_in, 16)
            act.dma_start(be_bc[:, :, :].rearrange("p e n -> p (e n)"),
                          b_e.rearrange("(a e) n -> a (e n)", a=1).to_broadcast((P, E * L))).then_inc(be_in, 16)

            def step1(g, j):
                a = g + 2
                if live(a, NG):
                    wait(act, xT_done, a + 1)
                    wait(act, ph_done, a - 1)
                    act.copy(ring_a[:, a_par(j + 2), :].rearrange("m (s q i) -> m q s i", s=SUB, q=PH),
                             ps_xT[:, :].rearrange("m (q s i) -> m q s i", q=PH, s=SUB)).then_inc(xT_ready, 1)
                a = g + 1
                if live(a, NG):
                    wait(act, ph_done, a + 1)
                    wait(act, conv_done, a - 1)
                    act.copy(phases[:, a_par(j + 1), :, 1:P + 1],
                             ps_ph[:, :].rearrange("k (s m) -> k s m", s=SUB)).then_inc(ph_ready, 1)
                a = g - 1
                if live(a, NG):
                    ja = (j - 1) % U
                    wait(act, tok_done, a + 1)
                    wait(act, scattered[ja], (a - ja) * (32 // U))
                    act.copy(htok[:, ja, :], ps_tok[:, :]).then_inc(tok_ready, 1)

            def a_par(j):
                return j % 2

            act.wait_ge(deq, N_DEQ)
            act.wait_ge(consts, N_CONSTS)
            stepped(act, step1, -2, lo1, hi1, NG + 1)

            act.wait_ge(mlp_in, 16 * 8)
            act.wait_ge(mlp_mm, 1)
            act.activation(g0[:, :], ps_misc[:, 0:N], ACT.Gelu, bias=b0_sb[:, 0:1]).then_inc(mlp_ev, 1)
            act.wait_ge(mlp_mm, 2)
            act.activation(g1[:, :], ps_misc[:, 0:N], ACT.Gelu, bias=b1_sb[:, 0:1]).then_inc(mlp_ev, 1)
            act.wait_ge(mlp_ev, 5)
            act.activation(att_x[:, :], att[:, :], ACT.Exp, accum_out=att_s[:, 0:1]).then_inc(mlp_ev, 1)
            act.wait_ge(mlp_ev, 11)
            act.dma_start(mixb_d, mixb_sb[:, :]).then_inc(mix_out, 16)
            act.dma_start(mix_d, mix_sb[:, :, :]).then_inc(mix_out, 16)

            def step2(s, j):
                a = s + 1
                if live(a, NT):
                    wait(act, lT_done, a + 1)
                    wait(act, exp_done, a - 1)
                    act.copy(hT[:, (j + 1) % 2, :], ps_lT[(j + 1) % 2][:, :]).then_inc(lT_ready, 1)
                a = s
                if live(a, NT):
                    wait(act, sum_ready, a + 1)
                    wait(act, result_out[j % 2], (a - j % 2) * 8)
                    act.activation(ring_b[:, j % 2, :], ring_a[:, j % 2, :], ACT.Relu, scale=0.5).then_inc(result_ready, 1)

            step2(-1, U - 1)
            step2(0, 0)
            act.wait_ge(mix_out, 32)
            act.dma_start(mixb_bc[:, :], mixb_d.rearrange("(a n) c -> a (n c)", a=1).to_broadcast((P, N * C))).then_inc(mix_in, 16)
            for s in range(SUB):
                rows = slice(s * C, (s + 1) * C)
                act.dma_start(mix_bd[rows, :, rows],
                              mix_d.rearrange("(g s) i o -> s i g o", s=SUB)[s]).then_inc(mix_in, 16)
            stepped(act, step2, 1, lo2, hi2, NT)

        @block.vector
        def _(dve):
            dve.wait_ge(convw_in, 16 * (C // CG))
            for s in range(SHIFTS):
                for p in range(PH):
                    k0 = PH * s - p + PH - 1
                    ins = dve.tensor_copy(wsel[:, s * PH + p, :, :], wfull[:, :, k0:k0 + PH].rearrange("o i q -> o q i"))
            ins.then_inc(wsel_ready, 1)
            dve.wait_ge(wT_done, 1)
            dve.tensor_copy(wconv[:, :, :, :].rearrange("k s p o -> k (s p o)"), bank[6][:, 0:SHIFTS * PH * C]).then_inc(wconv_ready, 1)
            dve.wait_ge(condT_done, 2)
            dve.tensor_copy(condT[:, :], ps_misc[:, 0:N]).then_inc(condT_ready, 1)
            dve.tensor_copy(cwT[:, :], ps_misc[:, N:N + C]).then_inc(condT_ready, 1)
            dve.wait_ge(ctx_mm, 1)
            dve.tensor_tensor(ctx_sb[:, :], ps_misc[:, 0:C], fs_bc[:, :], ALU.add).then_inc(ctx_ready, 1)

            words = htok[:, 0, :].bitcast(I32)
            half = wq[:, 0, :].bitcast(I32)
            deqs = [0]

            def deq_step(ins):
                deqs[0] += 1
                ins.then_inc(deq, 1)
                dve.wait_ge(deq, deqs[0])

            dve.wait_ge(consts, N_CONSTS)
            deq_step(dve.tensor_scalar(odd_i[:, :], lane_i[:, :], 1, None, ALU.bitwise_and))
            deq_step(dve.tensor_copy(odd[:, :], odd_i[:, :]))
            deq_step(dve.tensor_scalar(even[:, :], odd[:, :], -1.0, 1.0, ALU.mult, ALU.add))
            dve.wait_ge(q_in, 16 * 5)
            deq_step(dve.tensor_scalar(half, words, 16, None, ALU.logical_shift_right))
            deq_step(dve.tensor_scalar(ring_a[:, 0, :], half, odd[:, 0:1], None, ALU.mult))
            deq_step(dve.tensor_scalar(half, words, 65535, None, ALU.bitwise_and))
            deq_step(dve.scalar_tensor_tensor(words, half, even[:, 0:1], ring_a[:, 0, :], ALU.mult, ALU.add))
            for j in range(4):
                deq_step(dve.tensor_scalar(ring_a[:, 0, :].bitcast(I32), words, 4 * j, 15, ALU.logical_shift_right, ALU.bitwise_and))
                deq_step(dve.tensor_copy(ring_a[:, 1, :], ring_a[:, 0, :].bitcast(I32)))
                deq_step(dve.tensor_tensor(wq[:, j, :], ring_a[:, 1, :], scale_bc[:, :], ALU.mult))
                deq_step(dve.tensor_tensor(wq[:, j, :], wq[:, j, :], zero_bc[:, :], ALU.subtract))
            assert deqs[0] == N_DEQ
            dve.wait_ge(bg_in, 16)
            dve.wait_ge(ctx_in, 16)

            def step1(g, j):
                a, b = g - 1, g - 2
                ja, jb = (j - 1) % U, (j - 2) % U
                if live(g, NG):
                    wait(dve, conv_done, g + 1)
                    wait(dve, tok_done, g - 1)
                    dve.tensor_tensor(hT[:, j % 2, :].rearrange("m (p s o) -> m s p o", p=PH, s=SUB),
                                      ps_conv[j % 2][:, :].rearrange("m (s p o) -> m s p o", s=SUB, p=PH),
                                      ctx_bc[:, bass.ds(g * P, P)].rearrange("m (s a o) -> m s a o", s=SUB, a=1).to_broadcast((P, SUB, PH, C)),
                                      ALU.add).then_inc(hT_ready, 1)
                if live(a, NG):
                    wait(dve, gate_done, a + 1)
                    dve.tensor_tensor(logit[:, :], ps_gate[:, 0:E], bg_bc[:, :], ALU.add).then_inc(logit_ready, 1)
                if live(b, NG):
                    wait(dve, rank_done, b + 1)
                    wait(dve, base_ready, b)
                    dve.tensor_tensor(rank[:, :], ps_rank[:, 0:E], base[:, :], ALU.add).then_inc(rank_ready, 1)
                if live(a, NG):
                    wait(dve, logit_ready, a + 1)
                if live(b, NG):
                    wait(dve, rank_ready, b + 1)
                    dve.tensor_tensor(base[:, :], base[:, :], ps_rank[:, E:2 * E], ALU.add).then_inc(base_ready, 1)
                if live(a, NG):
                    dve.max(top[:, :], logit[:, :]).then_inc(top_ready, 1)
                    wait(dve, top_ready, a + 1)
                if live(b, NG):
                    for k in range(2):
                        dve.scalar_tensor_tensor(picked[:, k, :], iota_e[:, :], expert_of[:, bass.ds(b, 1), k:k + 1].rearrange("p a k -> p (a k)"),
                                                 rank[:, :], ALU.is_equal, ALU.mult,
                                                 accum_out=row_of[:, bass.ds(b, 1), k:k + 1].rearrange("p a k -> p (a k)")).then_inc(row_ready, 1)
                if live(a, NG):
                    dve.max_index(topi[:, :], top[:, :], logit[:, :]).then_inc(topi_ready, 1)
                if live(b, NG):
                    wait(dve, row_ready, 2 * b + 2)
                    wait(dve, scattered[jb], (b - jb) * (32 // U))
                    dve.tensor_scalar(row_i[:, jb, :], row_of[:, bass.ds(b, 1), :].rearrange("p a k -> p (a k)"), 0.0, None, ALU.add).then_inc(rowi_ready, 1)
                if live(a, NG):
                    wait(dve, topi_ready, a + 1)
                    dve.tensor_scalar(expert_of[:, bass.ds(a, 1), :].rearrange("p a k -> p (a k)"), topi[:, 0:2], 0.0, None, ALU.add).then_inc(expert_ready, 1)
                    wait(dve, expert_ready, a + 1)
                    e1, e2 = (expert_of[:, bass.ds(a, 1), k:k + 1].rearrange("p a k -> p (a k)") for k in range(2))
                    dve.tensor_scalar(chosen1[:, :], iota_e[:, :], e1, None, ALU.is_equal).then_inc(chosen1_ready, 1)
                    wait(dve, chosen1_ready, a + 1)
                    wait(dve, rank_done, a - 3)
                    dve.scalar_tensor_tensor(chosen[:, ja, :], iota_e[:, :], e2, chosen1[:, :], ALU.is_equal, ALU.add).then_inc(chosen_ready, 1)

            stepped(dve, step1, 0, lo1, hi1, NG + 2)

            n = [0]

            def then(ins):
                n[0] += 1
                ins.then_inc(table, 1)
                dve.wait_ge(table, n[0])

            dve.wait_ge(base_ready, NG)
            then(dve.tensor_copy(tail_i[0:1, :], base[0:1, :]))
            then(dve.scalar_tensor_tensor(tcount[:, :], base[:, :], float(P - 1), region[:, :], ALU.add, ALU.subtract))
            then(dve.tensor_copy(tint[:, :], tcount[:, :]))
            then(dve.tensor_scalar(tshift[:, :], tint[:, :], 7, None, ALU.logical_shift_right))
            then(dve.tensor_copy(prefix[:, 0, E:], tshift[:, :]))
            for k in range(3):
                then(dve.tensor_tensor(prefix[:, k + 1, E:], prefix[:, k, E:], prefix[:, k, E - (1 << k):2 * E - (1 << k)], ALU.add))
            then(dve.tensor_tensor(tstart[:, :], prefix[:, 3, E:], prefix[:, 0, E:], ALU.subtract))
            then(dve.scalar_tensor_tensor(offs[:, :], tstart[:, :], float(-P), region[:, :], ALU.mult, ALU.add))
            then(dve.tensor_copy(doffs[:, 0:1], offs[:, 0:1]))
            then(dve.tensor_tensor(doffs[:, 1:E], offs[:, 1:E], offs[:, 0:E - 1], ALU.subtract))
            then(dve.tensor_scalar(used[:, :], prefix[:, 3, 2 * E - 1:2 * E], lane[:, 0:1], None, ALU.is_gt))
            then(dve.tensor_scalar(mask[:, :], tstart[:, :], lane[:, 0:1], None, ALU.is_le))
            then(dve.tensor_tensor(mprod[:, :], mask[:, :], doffs[:, :], ALU.mult))
            then(dve.tensor_reduce(tsum[:, 0:1], mprod[:, :], AX.X, ALU.add))
            then(dve.tensor_reduce(tsum[:, 1:2], mask[:, :], AX.X, ALU.add))
            then(dve.scalar_tensor_tensor(tsum[:, 2:3], lane[:, :], float(P), tsum[:, 0:1], ALU.mult, ALU.add))
            then(dve.tensor_scalar(tsum[:, 3:4], tsum[:, 1:2], -1.0, None, ALU.add))
            then(dve.tensor_scalar(tab_f[:, 0:2], tsum[:, 2:4], used[:, 0:1], None, ALU.mult))
            dve.sem_inc(tab_ready, 1)
            dve.wait_ge(tab_done, 1)
            dve.tensor_copy(tab[:, :], ps_misc[0:2, 256:256 + P]).then_inc(tab_ready, 1)

            dve.wait_ge(mlp_mm, 3)
            dve.tensor_tensor(att_n[:, :], ps_misc[:, 0:E], b2_bc[:, :], ALU.add).then_inc(mlp_ev, 1)
            dve.wait_ge(mlp_ev, 3)
            dve.tensor_reduce(att_m[:, :], att_n[:, :], AX.X, ALU.max).then_inc(mlp_ev, 1)
            dve.wait_ge(mlp_ev, 4)
            dve.tensor_scalar(att[:, :], att_n[:, :], att_m[:, 0:1], None, ALU.subtract).then_inc(mlp_ev, 1)
            dve.wait_ge(mlp_ev, 6)
            dve.reciprocal(att_r[:, :], att_s[:, :]).then_inc(mlp_ev, 1)
            dve.wait_ge(mlp_ev, 7)
            dve.tensor_scalar(att_n[:, :], att_x[:, :], att_r[:, 0:1], None, ALU.mult).then_inc(mlp_ev, 1)
            dve.wait_ge(mlp_mm, 4)
            dve.tensor_copy(attT[:, :], ps_misc[0:E, 0:N]).then_inc(mlp_ev, 1)
            for k in range(2):
                dve.wait_ge(mlp_mm, 5 + k)
                src = ps_mix[k][:, :].rearrange("n (o i) -> n i o", i=C)
                ins = dve.tensor_copy(mix_sb[:, :, k * 16:k * 16 + 16], src)
                if k == 0:
                    ins.then_inc(mlp_ev, 1)
                    dve.wait_ge(mlp_mm, 7)
                    dve.tensor_copy(mixb_sb[:, :], ps_misc[:, 0:C])
                else:
                    ins.then_inc(mlp_ev, 1)

            rows2 = row_of[:, :, :].rearrange("p g k -> p (g k)")
            expert2 = expert_of[:, :, :].rearrange("p g k -> p (g k)")
            then(dve.tensor_scalar(shift_s[:, :], expert2, 0.0, offs[:, 0:1], ALU.is_equal, ALU.mult))
            for e in range(1, E):
                then(dve.tensor_scalar(shift_e[:, :], expert2, float(e), offs[:, e:e + 1], ALU.is_equal, ALU.mult))
                then(dve.tensor_tensor(shift_s[:, :], shift_s[:, :], shift_e[:, :], ALU.add))
            dve.tensor_tensor(place_i[:, :, :].rearrange("p g k -> p (g k)"), rows2, shift_s[:, :], ALU.subtract).then_inc(place_ready, 1)

            dve.wait_ge(be_in, 16)

            def step2(s, j):
                if live(s, NT):
                    expert = dve.value_load(tab[1:2, bass.ds(s, 1)], min_val=0, max_val=E - 1)
                    wait(dve, exp_done, s + 1)
                    wait(dve, result_ready, s - 1)
                    dve.tensor_tensor(ring_a[:, j % 2, :], ps_exp[j % 2][:, :],
                                      be_bc[:, bass.ds(expert, 1), :].rearrange("p a n -> p (a n)"), ALU.add).then_inc(sum_ready, 1)

            stepped(dve, step2, 0, lo2, hi2, NT)
            dve.wait_ge(mix_in, 16 * (1 + SUB))

            def step3(g, j):
                a = g + 2
                if live(a, NG):
                    ja = (j + 2) % U
                    wait(dve, x3_in[ja], ring_count(a, ja, XR))
                    wait(dve, gathered[ja % 2], (a - ja % 2) * 16 + 32)
                    wait(dve, mixed_done, a - 1)
                    wait(dve, yb_ready, a - 1)
                    dve.tensor_tensor(ring_a[:, ja % 2, :], xt[:, ja, :], htok[:, 2 * (ja % 2), :], ALU.add).then_inc(ya_ready, 1)
                b = g + 1
                if live(b, NG):
                    jb = (j + 1) % U
                    wait(dve, mixed_done, b + 1)
                    wait(dve, lin_done, b - 1)
                    dve.tensor_tensor(hT[:, jb % 2, :].rearrange("l (j t) -> l j t", j=4),
                                      ps_mix[jb % 2][:, :].rearrange("l (j t) -> l j t", j=4),
                                      mixb_bc[:, bass.ds(b * P, P)].rearrange("l (a t) -> l a t", a=1).to_broadcast((P, 4, P)),
                                      ALU.add).then_inc(mixed_ready, 1)
                if live(a, NG):
                    wait(dve, ya_ready, a + 1)
                    dve.tensor_tensor(ring_a[:, ja % 2, :], ring_a[:, ja % 2, :], htok[:, 2 * (ja % 2) + 1, :], ALU.add).then_inc(y_ready, 1)
                if live(g, NG):
                    wait(dve, lin_done, g + 1)
                    wait(dve, yb_ready, g + 1)
                    wait(dve, out_out[j % 2], (g - j % 2) * 8)
                    dve.tensor_tensor(orow[:, j % 2, :], ps_lin[j % 2][:, :], ring_b[:, j % 2, :], ALU.add).then_inc(out_ready, 1)

            stepped(dve, step3, -2, lo1, hi1, NG)

        @block.tensor
        def _(pe):
            pe.wait_ge(consts, 5)
            pe.wait_ge(wsel_ready, 1)
            for s in range(SHIFTS):
                for p in range(PH):
                    at = (s * PH + p) * C
                    mm = pe.transpose(bank[6][:, at:at + C],
                                      wsel[:, s * PH + p, :, :].rearrange("o q i -> o (q i)"), ident[0:C, 0:C])
            mm.then_inc(wT_done, 1)
            pe.wait_ge(cond_in, 48)
            pe.transpose(ps_misc[:, 0:N], cond_sb[:, :], ident[:, :]).then_inc(condT_done, 1)
            pe.transpose(ps_misc[:, N:N + C], cw_sb[:, :], ident[0:C, 0:C]).then_inc(condT_done, 1)
            pe.wait_ge(condT_ready, 2)
            pe.matmul(ps_misc[:, 0:C], condT[:, :], cwT[:, :], start=True, stop=True).then_inc(ctx_mm, 1)

            def step1(g, j):
                a = g + 2
                if live(a, NG):
                    ja = (j + 2) % U
                    wait(pe, x_in[ja], ring_count(a, ja, XR))
                    wait(pe, xT_ready, a)
                    for q in range(PH):
                        mm = pe.transpose(ps_xT[:, q * P:(q + 1) * P],
                                          xt[:, ja, q:L:PH], ident[:, :])
                    mm.then_inc(xT_done, 1)
                if live(g, NG):
                    wait(pe, ph_ready, g + 1)
                    wait(pe, hT_ready, g - 1)
                    if isinstance(g, int) and g == 0:
                        pe.wait_ge(wconv_ready, 1)
                    for s in range(SUB):
                        for t in range(SHIFTS):
                            mm = pe.matmul(ps_conv[j % 2][:, s * P:(s + 1) * P], phases[:, j % 2, s, t:t + P],
                                           wconv[:, t, :, :].rearrange("k p o -> k (p o)"),
                                           start=(t == 0), stop=(t == SHIFTS - 1))
                    mm.then_inc(conv_done, 1)
                a = g + 1
                if live(a, NG):
                    wait(pe, xT_ready, a + 1)
                    wait(pe, ph_ready, a)
                    for s in range(SUB):
                        mm = pe.transpose(ps_ph[:, s * P:(s + 1) * P], ring_a[:, (j + 1) % 2, s * P:(s + 1) * P], ident[:, :])
                    mm.then_inc(ph_done, 1)
                a = g - 1
                if live(a, NG):
                    ja = (j - 1) % U
                    wait(pe, hT_ready, a + 1)
                    wait(pe, logit_ready, a)
                    if isinstance(a, int) and a == 0:
                        pe.wait_ge(gate_in, 16)
                        pe.wait_ge(consts, N_CONSTS)
                    for p in range(PH):
                        mm = pe.matmul(ps_gate[:, 0:P], hT[:, ja % 2, p * P:(p + 1) * P], wg[:, p, :],
                                       start=(p == 0), stop=(p == PH - 1))
                    mm.then_inc(gate_done, 1)
                    wait(pe, tok_ready, a)
                    for p in range(PH):
                        mm = pe.transpose(ps_tok[:, p * P:(p + 1) * P], hT[:, ja % 2, p * P:(p + 1) * P], ident[:, :])
                    mm.then_inc(tok_done, 1)
                a = g - 2
                if live(a, NG):
                    ja = (j - 2) % U
                    wait(pe, chosen_ready, a + 1)
                    wait(pe, base_ready, a)
                    pe.matmul(ps_rank[:, 0:E], before[:, :], chosen[:, ja, :], start=True, stop=True)
                    pe.matmul(ps_rank[:, E:2 * E], ones[:, :], chosen[:, ja, :], start=True, stop=True).then_inc(rank_done, 1)

            stepped(pe, step1, -2, lo1, hi1, NG + 2)

            pe.wait_ge(mlp_in, 16 * 8)
            pe.matmul(ps_misc[:, 0:N], w0_sb[:, :], condT[:, :], start=True, stop=True).then_inc(mlp_mm, 1)
            pe.wait_ge(mlp_ev, 1)
            pe.matmul(ps_misc[:, 0:N], w1_sb[:, :], g0[:, :], start=True, stop=True).then_inc(mlp_mm, 1)
            pe.wait_ge(mlp_ev, 2)
            pe.wait_ge(tab_ready, 1)
            pe.transpose(ps_misc[0:2, 256:256 + P], tab_f[:, :], ident[:, :]).then_inc(tab_done, 1)
            pe.wait_ge(tab_ready, 2)
            pe.matmul(ps_misc[:, 0:E], g1[:, :], w2_sb[:, :], start=True, stop=True).then_inc(mlp_mm, 1)
            pe.wait_ge(mlp_ev, 8)
            pe.transpose(ps_misc[0:E, 0:N], att_n[:, :], ident[:, :]).then_inc(mlp_mm, 1)
            pe.wait_ge(mlp_ev, 9)
            for k in range(2):
                pe.matmul(ps_mix[k][:, :], attT[:, :], mixw_sb[:, k * 512:(k + 1) * 512], start=True, stop=True).then_inc(mlp_mm, 1)
            pe.matmul(ps_misc[:, 0:C], attT[:, :], mixb_w[:, :], start=True, stop=True).then_inc(mlp_mm, 1)
            pe.wait_ge(we_in, 16 * E)

            def step2(s, j):
                a = s + 1
                if live(a, NT):
                    ja = (j + 1) % U
                    wait(pe, list_in[ja], ring_count(a, ja, U))
                    wait(pe, lT_ready, a - 1)
                    for p in range(PH):
                        mm = pe.transpose(ps_lT[ja % 2][:, p * P:(p + 1) * P], htok[:, ja, p * P:(p + 1) * P], ident[:, :])
                    mm.then_inc(lT_done, 1)
                if live(s, NT):
                    expert = pe.value_load(tab[1:2, bass.ds(s, 1)], min_val=0, max_val=E - 1)
                    wait(pe, lT_ready, s + 1)
                    wait(pe, sum_ready, s - 1)
                    for p in range(PH):
                        mm = pe.matmul(ps_exp[j % 2][:, :], hT[:, j % 2, p * P:(p + 1) * P],
                                       we[:, bass.ds(expert, 1), p, :].rearrange("m a n -> m (a n)"),
                                       start=(p == 0), stop=(p == PH - 1))
                    mm.then_inc(exp_done, 1)

            stepped(pe, step2, -1, lo2, hi2, NT)
            pe.wait_ge(mix_in, 16 * (1 + SUB))
            pe.wait_ge(deq, N_DEQ)

            def step3(g, j):
                a = g + 1
                if live(a, NG):
                    ja = (j + 1) % 2
                    wait(pe, y_ready, a + 1)
                    wait(pe, mixed_ready, a - 1)
                    for q in range(4):
                        cols = ring_a[:, ja, q:L:4]
                        mm = pe.matmul(ps_mix[ja][:, q * P:(q + 1) * P], cols,
                                       mix_bd[:, bass.ds(a, 1), :].rearrange("c a t -> c (a t)"), start=True, stop=True)
                    mm.then_inc(mixed_done, 1)
                if live(g, NG):
                    wait(pe, mixed_ready, g + 1)
                    wait(pe, out_ready, g - 1)
                    for q in range(4):
                        mm = pe.matmul(ps_lin[j % 2][:, :], hT[:, j % 2, q * P:(q + 1) * P], wq[:, q, :],
                                       start=(q == 0), stop=(q == 3))
                    mm.then_inc(lin_done, 1)

            stepped(pe, step3, -1, lo1, hi1, NG)


_INS = ['x', 'cond_128', 'fside_S_0', 'L0_cond_weight', 'L0_cond_c_weight', 'L0_ffn_W_gate', 'L0_ffn_b_gate',
        'L0_ffn_W_e', 'L0_ffn_b_e', 'L1_cond_W0', 'L1_cond_b0', 'L1_cond_W1', 'L1_cond_b1', 'L1_cond_W2',
        'L1_cond_b2', 'L1_cond_weight', 'L1_cond_bias_k', 'L1_ffn_qweight', 'L1_ffn_scales', 'L1_ffn_zeros',
        'L1_ffn_bias']


def kernel(**inputs):
    import concourse.bacc as bacc
    from concourse.bass_utils import run_bass_kernel_spmd

    nc = bacc.Bacc("TRN2", target_bir_lowering=False, num_devices=1)
    arrays, args = {}, []
    for name in _INS:
        a = np.ascontiguousarray(inputs[name])
        arrays[f"in_{name}"] = a
        args.append(nc.dram_tensor(f"in_{name}", a.shape, mybir.dt.from_np(a.dtype), kind="ExternalInput").ap())
    result = nc.dram_tensor("out", (N, C, L), F32, kind="ExternalOutput").ap()
    build_program(nc, *args, result)
    r = run_bass_kernel_spmd(nc, [arrays], core_ids=[0])
    return r.results[0]["out"]
```

```python
from contextlib import ExitStack

import numpy as np

import concourse.bass as bass
from concourse import mybir

F32 = mybir.dt.float32
BF16 = mybir.dt.bfloat16
I32 = mybir.dt.int32
U32 = mybir.dt.uint32
ALU = mybir.AluOpType
ACT = mybir.ActivationFunctionType
AX = mybir.AxisListType

P = 128
N, C, L = 128, 32, 512
SUB = P // C
NG = N // SUB
TAPS, PAD, CG = 9, 4, 8
PH = L // P
B = 32
MH = P // B
SHIFTS = 3
KW = TAPS + 2 * (PH - 1)
E = 8
REGION = N * C + P
NT = (2 * N * C - E) // P + E
U = 4
XR = 4


def live(i, n):
    return not isinstance(i, int) or 0 <= i < n


def wait(eng, sem, value):
    if not isinstance(value, int) or value > 0:
        eng.wait_ge(sem, value)


def stepped(eng, step, first, lo, hi, last):
    assert (hi - lo) % U == 0 and lo % U == 0
    for i in range(first, lo):
        step(i, i % U)
    with eng.Fori(0, (hi - lo) // U) as k:
        base = k * U + lo
        for j in range(U):
            step(base + j, j)
    for i in range(hi, last):
        step(i, i % U)


def ring_count(i, j, ring):
    return (i - j % ring) * (16 // ring) + 16


def build_program(nc, x, cond, fside, conv_w, ctx_w, w_gate, b_gate, w_e, b_e,
                  w0, b0, w1, b1, w2, b2, mix_w, mix_b, qweight, scales, zeros, bias, out):
    ctx = ExitStack()
    with ctx:
        def sb(name, shape, dt=F32):
            return ctx.enter_context(nc.sbuf_tensor(name, shape, dt))

        def sem(name):
            return ctx.enter_context(nc.semaphore(name))

        def dram(name, shape):
            return nc.dram_tensor(name, shape, F32, kind="Internal").ap()

        lists_d = dram("lists_d", (E * REGION, L))
        result_d = dram("result_d", (NT * P, L))
        ctx_d = dram("ctx_d", (N, C))
        mixb_d = dram("mixb_d", (N, C))
        mix_d = dram("mix_d", (N, C, C))

        x_g = x.rearrange("(g s) c l -> g (s c) l", s=SUB)
        out_g = out.rearrange("(g s) c l -> g (s c) l", s=SUB)

        we = sb("we", [P, E, PH, L])
        be_bc = sb("be_bc", [P, E, L])
        ctx_bc = sb("ctx_bc", [P, N * C])
        mixb_bc = sb("mixb_bc", [P, N * C])
        mix_bd = sb("mix_bd", [P, NG, P])
        wq = sb("wq", [P, 4, L])
        scale_bc = sb("scale_bc", [P, L])
        zero_bc = sb("zero_bc", [P, L])
        bias_bc = sb("bias_bc", [P, L])
        xt = sb("xt", [P, XR, L])
        ring_a = sb("ring_a", [P, 2, L])
        phases = sb("phases", [P, 2, SUB, P + 2])
        hT = sb("hT", [P, 2, L])
        htok = sb("htok", [P, U, L])
        ring_b = sb("ring_b", [P, 2, L])
        orow = sb("orow", [P, 2, L])
        ident = sb("ident", [P, P])
        before = sb("before", [P, P], BF16)
        ones = sb("ones", [P, P], BF16)
        wconv = sb("wconv", [P, SHIFTS, PH, C])
        wfull = sb("wfull", [C, C, KW])
        wg = sb("wg", [P, PH, P])
        bg_bc = sb("bg_bc", [P, E])
        iota_e = sb("iota_e", [P, E])
        region = sb("region", [P, E])
        lane = sb("lane", [P, 1])
        base = sb("base", [P, E])
        logit = sb("logit", [P, E])
        top = sb("top", [P, E])
        topi = sb("topi", [P, E], U32)
        chosen1 = sb("chosen1", [P, E])
        chosen = sb("chosen", [P, U, E], BF16)
        rank = sb("rank", [P, E])
        picked = sb("picked", [P, 2, E])
        expert_of = sb("expert_of", [P, NG, 2])
        row_of = sb("row_of", [P, NG, 2])
        row_i = sb("row_i", [P, U, 2], I32)
        tcount = sb("tcount", [P, E])
        tint = sb("tint", [P, E], I32)
        tshift = sb("tshift", [P, E], I32)
        prefix = sb("prefix", [P, 4, 2 * E])
        tstart = sb("tstart", [P, E])
        offs = sb("offs", [P, E])
        doffs = sb("doffs", [P, E])
        mask = sb("mask", [P, E])
        mprod = sb("mprod", [P, E])
        tsum = sb("tsum", [P, 4])
        used = sb("used", [P, 1])
        tab_f = sb("tab_f", [P, 2])
        tab = sb("tab", [2, P], I32)
        tail_i = sb("tail_i", [1, E], I32)
        shift_e = sb("shift_e", [P, NG * 2])
        shift_s = sb("shift_s", [P, NG * 2])
        place_i = sb("place_i", [P, NG, 2], I32)
        gidx = sb("gidx", [P, 2, 2], I32)
        cond_sb = sb("cond_sb", [N, P])
        condT = sb("condT", [P, N])
        cw_sb = sb("cw_sb", [C, P])
        cwT = sb("cwT", [P, C])
        fs_bc = sb("fs_bc", [P, C])
        ctx_sb = sb("ctx_sb", [N, C])
        w0_sb = sb("w0_sb", [P, P])
        w1_sb = sb("w1_sb", [P, P])
        w2_sb = sb("w2_sb", [P, E])
        b0_sb = sb("b0_sb", [P, 1])
        b1_sb = sb("b1_sb", [P, 1])
        b2_bc = sb("b2_bc", [P, E])
        mixb_w = sb("mixb_w", [E, C])
        g0 = sb("g0", [P, N])
        g1 = sb("g1", [P, N])
        att = sb("att", [N, E])
        att_m = sb("att_m", [N, 1])
        att_x = sb("att_x", [N, E])
        att_s = sb("att_s", [N, 1])
        att_r = sb("att_r", [N, 1])
        att_n = sb("att_n", [N, E])
        attT = sb("attT", [E, N])
        mixb_sb = sb("mixb_sb", [N, C])
        mixw_sb = ring_b[0:E, :, :].rearrange("k h n -> k (h n)")
        mix_sb = sb("mix_sb", [N, C, C])
        wsel = htok[0:C, 1:4, :].rearrange("o a (b q i) -> o (a b) q i", q=PH, i=C)
        words = sb("words", [P, L], I32)
        lane_i = sb("lane_i", [P, 1], I32)
        odd_i = sb("odd_i", [P, 1], I32)
        odd = sb("odd", [P, 1])
        even = sb("even", [P, 1])

        bank = [ctx.enter_context(nc.psum_tensor(f"bank{i}", [P, 512], F32)) for i in range(8)]
        ps_ph, ps_conv, ps_tok, ps_gate, ps_rank, ps_misc = (
            bank[1], bank[2:4], bank[4], bank[5], bank[6], bank[7])
        ps_exp = bank[2:4]
        ps_mix, ps_lin = bank[4:6], bank[2:4]

        ident_ready = sem("ident_ready")
        pads_ready = sem("pads_ready")
        consts = sem("consts")
        mixbd_zero = sem("mixbd_zero")
        wfull_zero = sem("wfull_zero")
        convw_in = sem("convw_in")
        cond_in = sem("cond_in")
        fs_in = sem("fs_in")
        gate_in = sem("gate_in")
        bg_in = sem("bg_in")
        mlp_in = sem("mlp_in")
        q_in = sem("q_in")
        be_in = sem("be_in")
        we_in = sem("we_in")
        x_in = [sem(f"x_in{i}") for i in range(XR)]
        wsel_ready = sem("wsel_ready")
        wT_done = sem("wT_done")
        wconv_ready = sem("wconv_ready")
        condT_done = sem("condT_done")
        condT_ready = sem("condT_ready")
        ctx_mm = sem("ctx_mm")
        ctx_ready = sem("ctx_ready")
        ctx_out = sem("ctx_out")
        ctx_in = [sem(f"ctx_in{i}") for i in range(2)]
        deq = sem("deq")
        xT_ready = sem("xT_ready")
        ph_done = sem("ph_done")
        ph_ready = sem("ph_ready")
        conv_done = sem("conv_done")
        hT_ready = sem("hT_ready")
        gate_done = sem("gate_done")
        tok_done = sem("tok_done")
        tok_ready = sem("tok_ready")
        logit_ready = sem("logit_ready")
        top_ready = sem("top_ready")
        topi_ready = sem("topi_ready")
        expert_ready = sem("expert_ready")
        chosen1_ready = sem("chosen1_ready")
        chosen_ready = sem("chosen_ready")
        rank_done = sem("rank_done")
        rank_ready = sem("rank_ready")
        base_ready = sem("base_ready")
        row_ready = sem("row_ready")
        rowi_ready = sem("rowi_ready")
        scatter_go = sem("scatter_go")
        scattered = [sem(f"scattered{i}") for i in range(U)]
        table = sem("table")
        tab_done = sem("tab_done")
        tab_ready = sem("tab_ready")
        tail_out = sem("tail_out")
        place_ready = sem("place_ready")
        mlp_mm = sem("mlp_mm")
        mlp_ev = sem("mlp_ev")
        mix_out = sem("mix_out")
        mix_in = sem("mix_in")
        list_in = [sem(f"list_in{i}") for i in range(U)]
        lT_ready = sem("lT_ready")
        exp_done = sem("exp_done")
        sum_ready = sem("sum_ready")
        result_ready = sem("result_ready")
        result_out = [sem(f"result_out{i}") for i in range(2)]
        gidx_ready = sem("gidx_ready")
        gather_go = sem("gather_go")
        gathered = [sem(f"gathered{i}") for i in range(2)]
        x3_in = [sem(f"x3_in{i}") for i in range(XR)]
        ya_ready = sem("ya_ready")
        y_ready = sem("y_ready")
        mixed_done = sem("mixed_done")
        mixed_ready = sem("mixed_ready")
        yb_ready = sem("yb_ready")
        lin_done = sem("lin_done")
        out_ready = sem("out_ready")
        out_out = [sem(f"out_out{i}") for i in range(2)]

        N_CONSTS = 11
        N_DEQ = 7 + 4 * 3
        CTX_FIRST = 2 * P
        zeros_t = orow[:, 0, :]
        lo1, hi1 = U, NG - U
        lo2, hi2 = 2 * U, NT // U * U

        block = ctx.enter_context(nc.Block())

        @block.sync
        def _(sp):
            sp.dma_start(cond_sb[:, :], cond).then_inc(cond_in, 16)
            sp.dma_start(cw_sb[:, :], ctx_w).then_inc(cond_in, 16)
            sp.dma_start(xt[:, 0, :], x_g[0]).then_inc(x_in[0], 16)
            sp.wait_ge(wfull_zero, 1)
            for s in range(C // CG):
                rows = slice(s * CG, (s + 1) * CG)
                sp.dma_start(wfull[rows, rows, PH - 1:PH - 1 + TAPS], conv_w[rows]).then_inc(convw_in, 16)
            for g in range(1, XR):
                sp.dma_start(xt[:, g, :], x_g[g]).then_inc(x_in[g], 16)
            sp.wait_ge(ctx_ready, 1)
            sp.dma_start(ctx_d, ctx_sb[:, :]).then_inc(ctx_out, 16)
            sp.wait_ge(ctx_out, 16)
            ctx_row = ctx_d.rearrange("(a n) c -> a (n c)", a=1)
            for i, cols in enumerate((slice(0, CTX_FIRST), slice(CTX_FIRST, N * C))):
                sp.dma_start(ctx_bc[:, cols], ctx_row[:, cols].to_broadcast((P, cols.stop - cols.start))).then_inc(ctx_in[i], 16)

            def load_we(e):
                return sp.dma_start(we[:, bass.ds(e, 1), :, :].rearrange("m a p n -> m (a p n)"),
                                    w_e[bass.ds(e, 1)].rearrange("a (m p) n -> m (a p n)", p=PH)).then_inc(we_in, 16)

            load_we(0)
            with sp.Fori(0, NG // XR - 1) as k:
                for j in range(XR):
                    sp.wait_ge(xT_ready, k * XR + j + 1)
                    sp.dma_start(xt[:, j, :], x_g[bass.ds(k * XR + XR + j, 1)].rearrange("a p l -> p (a l)")).then_inc(x_in[j], 16)
                load_we(k + 1)

            sp.wait_ge(table, 1)
            ends = [sp.alloc_register(f"end{e}") for e in range(E)]
            sp.load(ends, tail_i[0:1, :])
            for e in range(E):
                end = sp.snap(ends[e], min_val=e * REGION, max_val=(e + 1) * REGION - P)
                sp.dma_start(lists_d[bass.ds(end, P), :], zeros_t).then_inc(tail_out, 16)
            for s in scattered:
                sp.wait_ge(s, 32 * (NG // U))
            sp.wait_ge(tail_out, 16 * E)
            sp.wait_ge(tab_ready, 2)
            row_reg = sp.alloc_register("row_reg")

            def list_step(s, j):
                a = s + 3
                if live(a, NT):
                    ja = (j + 3) % U
                    sp.reg_load(row_reg, tab[0:1, bass.ds(a, 1)])
                    row = sp.snap(row_reg, min_val=0, max_val=E * REGION - P)
                    wait(sp, lT_ready, a - 3)
                    for mh in range(MH):
                        sp.dma_start(htok[mh * B:(mh + 1) * B, ja, :].rearrange("r (h n) -> r h n", h=MH),
                                     lists_d[bass.ds(row, P), mh * P:(mh + 1) * P].rearrange("(h r) n -> r h n", r=B)
                                     ).then_inc(list_in[ja], 16)

            stepped(sp, list_step, -3, lo2, hi2 - U, NT - 3)

            def row_step(g, j):
                a = g + 3
                if live(a, NG):
                    ja = (j + 3) % U
                    wait(sp, ya_ready, a - 3)
                    sp.dma_start(xt[:, ja, :], x_g[bass.ds(a, 1)].rearrange("a p l -> p (a l)")).then_inc(x3_in[ja], 16)
                if live(g, NG):
                    wait(sp, out_ready, g + 1)
                    sp.dma_start(out_g[bass.ds(g, 1)].rearrange("a p l -> p (a l)"), orow[:, j % 2, :]).then_inc(out_out[j % 2], 16)

            stepped(sp, row_step, -3, lo1, hi1, NG)
            for s in out_out:
                sp.wait_ge(s, 16 * (NG // 2))

        @block.gpsimd
        def _(pool):
            pool.memset(ident[:, :], 0.0).then_inc(ident_ready, 1)
            pool.wait_ge(ident_ready, 1)
            pool.affine_select(out=ident[:, :], in_=ident[:, :], compare_op=ALU.not_equal, fill=1.0, base=0,
                               pattern=[[-1, P]], channel_multiplier=1).then_inc(ident_ready, 1)
            for edge in (0, P + 1):
                pool.memset(phases[:, :, :, edge:edge + 1], 0.0).then_inc(pads_ready, 1)
            pool.memset(wg[:, :, :], 0.0).then_inc(consts, 1)
            pool.memset(before[:, :], 1.0).then_inc(consts, 1)
            pool.wait_ge(consts, 2)
            pool.dma_start(wg[:, :, 0:E], w_gate.rearrange("(m p) e -> m p e", p=PH)).then_inc(gate_in, 16)
            pool.affine_select(out=before[:, :], in_=before[:, :], compare_op=ALU.is_ge, fill=0.0, base=-1,
                               pattern=[[1, P]], channel_multiplier=-1).then_inc(consts, 1)
            pool.memset(ones[:, :], 1.0).then_inc(consts, 1)
            exact = dict(allow_small_or_imprecise_dtypes=True)
            pool.iota(iota_e[:, :], pattern=[[1, E]], base=0, channel_multiplier=0, **exact).then_inc(consts, 1)
            pool.iota(region[:, :], pattern=[[REGION, E]], base=0, channel_multiplier=0, **exact).then_inc(consts, 1)
            pool.iota(base[:, :], pattern=[[REGION, E]], base=0, channel_multiplier=0, **exact).then_inc(consts, 1)
            pool.iota(lane[:, :], pattern=[[0, 1]], base=0, channel_multiplier=1, **exact).then_inc(consts, 1)
            pool.iota(lane_i[:, :], pattern=[[0, 1]], base=0, channel_multiplier=1).then_inc(consts, 1)
            pool.memset(prefix[:, :, :], 0.0).then_inc(consts, 1)
            pool.memset(zeros_t, 0.0).then_inc(consts, 1)
            for dst, src in ((w0_sb[:, :], w0), (w1_sb[:, :], w1), (w2_sb[:, :], w2),
                             (b0_sb[:, :], b0.rearrange("(n a) -> n a", a=1)),
                             (b1_sb[:, :], b1.rearrange("(n a) -> n a", a=1)),
                             (b2_bc[:, :], b2.rearrange("(a e) -> a e", a=1).to_broadcast((P, E))),
                             (mixw_sb, mix_w.rearrange("k o i a -> k (o i a)")),
                             (mixb_w[:, :], mix_b)):
                pool.dma_start(dst, src).then_inc(mlp_in, 16)
            pool.memset(mix_bd[:, :, :], 0.0).then_inc(mixbd_zero, 1)

            def scatter_step(g, j):
                wait(pool, tok_ready, g + 1)
                wait(pool, rowi_ready, g + 1)
                pool.sem_inc(scatter_go, 1)
                for k in range(2):
                    pool.indirect_dma_start(lists_d, bass.IndirectOffsetOnAxis(ap=row_i[:, j, k:k + 1], axis=0),
                                            htok[:, j, :], None, bounds_check=E * REGION - 1,
                                            oob_is_err=False).then_inc(scattered[j], 16)

            stepped(pool, scatter_step, 0, lo1, hi1, NG)

            for i, s in enumerate(result_out):
                pool.wait_ge(s, 16 * ((NT + 1 - i) // 2))
            pool.wait_ge(place_ready, 1)

            def gather(g, j):
                wait(pool, gathered[j % 2], (g - j % 2) * 16)
                wait(pool, y_ready, g - 1)
                pool.sem_inc(gather_go, 1)
                pool.tensor_copy(gidx[:, j % 2, :], place_i[:, bass.ds(g, 1), :].rearrange("p a k -> p (a k)")).then_inc(gidx_ready, 1)
                wait(pool, gidx_ready, g + 1)
                pool.sem_inc(gather_go, 1)
                for k in range(2):
                    pool.indirect_dma_start(htok[:, 2 * (j % 2) + k, :], None, result_d,
                                            bass.IndirectOffsetOnAxis(ap=gidx[:, j % 2, k:k + 1], axis=0),
                                            bounds_check=NT * P - 1, oob_is_err=False).then_inc(gathered[j % 2], 16)

            def bias_add(g, j):
                wait(pool, y_ready, g + 1)
                wait(pool, out_ready, g - 1)
                pool.tensor_tensor(ring_b[:, j % 2, :], ring_a[:, j % 2, :], bias_bc[:, :], ALU.add).then_inc(yb_ready, 1)

            def step3(g, j):
                if live(g + 2, NG):
                    gather(g + 2, (j + 2) % U)
                if live(g, NG):
                    bias_add(g, j)

            stepped(pool, step3, -2, lo1, hi1, NG)

        @block.scalar
        def _(act):
            act.dma_start(fs_bc[:, :], fside.rearrange("(a c) -> a c", a=1).to_broadcast((P, C))).then_inc(fs_in, 16)
            act.dma_start(bg_bc[:, :], b_gate.rearrange("(a e) -> a e", a=1).to_broadcast((P, E))).then_inc(bg_in, 16)
            act.wait_ge(convw_in, 16 * (C // CG))
            for u in range(2):
                act.dma_start(words[u:P:2, :], qweight).then_inc(q_in, 16)
            act.dma_start(scale_bc[:, :], scales.rearrange("n a -> a n").to_broadcast((P, L))).then_inc(q_in, 16)
            act.dma_start(zero_bc[:, :], zeros.rearrange("n a -> a n").to_broadcast((P, L))).then_inc(q_in, 16)
            act.dma_start(bias_bc[:, :], bias.rearrange("(a n) -> a n", a=1).to_broadcast((P, L))).then_inc(q_in, 16)
            act.dma_start(be_bc[:, :, :].rearrange("p e n -> p (e n)"),
                          b_e.rearrange("(a e) n -> a (e n)", a=1).to_broadcast((P, E * L))).then_inc(be_in, 16)

            def step1(g, j):
                a = g + 1
                if live(a, NG):
                    wait(act, ph_done, a + 1)
                    wait(act, conv_done, a - 1)
                    act.copy(phases[:, (j + 1) % 2, :, 1:P + 1].rearrange("k s (h l) -> k h s l", h=MH),
                             ps_ph[:, :].rearrange("k (h s l) -> k h s l", h=MH, s=SUB)).then_inc(ph_ready, 1)
                a = g - 1
                if live(a, NG):
                    ja = (j - 1) % U
                    wait(act, tok_done, a + 1)
                    wait(act, scattered[ja], (a - ja) * (32 // U))
                    act.copy(htok[:, ja, :].rearrange("t (h p l) -> t p h l", h=MH, p=PH),
                             ps_tok[:, :].rearrange("t (p h l) -> t p h l", p=PH, h=MH)).then_inc(tok_ready, 1)

            act.wait_ge(pads_ready, 2)
            stepped(act, step1, -1, lo1, hi1, NG + 1)

            act.wait_ge(mlp_in, 16 * 8)
            act.wait_ge(mlp_mm, 1)
            act.activation(g0[:, :], ps_misc[:, 0:N], ACT.Gelu, bias=b0_sb[:, 0:1]).then_inc(mlp_ev, 1)
            act.wait_ge(mlp_mm, 2)
            act.activation(g1[:, :], ps_misc[:, 0:N], ACT.Gelu, bias=b1_sb[:, 0:1]).then_inc(mlp_ev, 1)
            act.wait_ge(mlp_ev, 5)
            act.activation(att_x[:, :], att[:, :], ACT.Exp, accum_out=att_s[:, 0:1]).then_inc(mlp_ev, 1)
            act.wait_ge(mlp_ev, 11)
            act.dma_start(mixb_d, mixb_sb[:, :]).then_inc(mix_out, 16)
            act.dma_start(mix_d, mix_sb[:, :, :]).then_inc(mix_out, 16)

            def step2(s, j):
                a = s
                if live(a, NT):
                    wait(act, sum_ready, a + 1)
                    wait(act, result_out[j % 2], (a - j % 2) * 8)
                    act.activation(ring_b[:, j % 2, :], ring_a[:, j % 2, :], ACT.Relu, scale=0.5).then_inc(result_ready, 1)
                    wait(act, result_ready, a + 1)
                    act.dma_start(result_d[bass.ds(a * P, P), :], ring_b[:, j % 2, :]).then_inc(result_out[j % 2], 16)

            step2(0, 0)
            act.wait_ge(mixbd_zero, 1)
            act.wait_ge(mix_out, 32)
            act.dma_start(mixb_bc[:, :], mixb_d.rearrange("(a n) c -> a (n c)", a=1).to_broadcast((P, N * C))).then_inc(mix_in, 16)
            for s in range(SUB):
                rows = slice(s * C, (s + 1) * C)
                act.dma_start(mix_bd[rows, :, rows],
                              mix_d.rearrange("(g s) i o -> s i g o", s=SUB)[s]).then_inc(mix_in, 16)
            stepped(act, step2, 1, lo2, hi2, NT)

        @block.vector
        def _(dve):
            dve.memset(wfull[:, :, :], 0.0).then_inc(wfull_zero, 1)
            dve.wait_ge(condT_done, 2)
            dve.tensor_copy(condT[:, :], ps_misc[:, 0:N]).then_inc(condT_ready, 1)
            dve.tensor_copy(cwT[:, :], ps_misc[:, N:N + C]).then_inc(condT_ready, 1)
            dve.wait_ge(ctx_mm, 1)
            dve.wait_ge(fs_in, 16)
            dve.tensor_tensor(ctx_sb[:, :], ps_misc[:, 0:C], fs_bc[:, :], ALU.add).then_inc(ctx_ready, 1)
            dve.wait_ge(convw_in, 16 * (C // CG))
            for s in range(SHIFTS):
                for p in range(PH):
                    k0 = PH * s - p + PH - 1
                    ins = dve.tensor_copy(wsel[:, s * PH + p, :, :], wfull[:, :, k0:k0 + PH].rearrange("o i q -> o q i"))
            ins.then_inc(wsel_ready, 1)
            dve.wait_ge(wT_done, 1)
            dve.tensor_copy(wconv[:, :, :, :].rearrange("k s p o -> k (s p o)"), bank[6][:, 0:SHIFTS * PH * C]).then_inc(wconv_ready, 1)

            deqs = [0]

            def deq_step(ins):
                deqs[0] += 1
                ins.then_inc(deq, 1)
                dve.wait_ge(deq, deqs[0])

            def pick_halves():
                half = wq[:, 0, :].bitcast(I32)
                odd_part = wq[:, 1, :]
                deq_step(dve.tensor_scalar(odd_i[:, :], lane_i[:, :], 1, None, ALU.bitwise_and))
                deq_step(dve.tensor_copy(odd[:, :], odd_i[:, :]))
                deq_step(dve.tensor_scalar(even[:, :], odd[:, :], -1.0, 1.0, ALU.mult, ALU.add))
                dve.wait_ge(q_in, 16 * 5)
                deq_step(dve.tensor_scalar(half, words[:, :], 16, None, ALU.logical_shift_right))
                deq_step(dve.tensor_scalar(odd_part, half, odd[:, 0:1], None, ALU.mult))
                deq_step(dve.tensor_scalar(half, words[:, :], 65535, None, ALU.bitwise_and))
                deq_step(dve.scalar_tensor_tensor(words[:, :], half, even[:, 0:1], odd_part, ALU.mult, ALU.add))

            def dequantize(j):
                nibble = orow[:, 1, :].bitcast(I32)
                deq_step(dve.tensor_scalar(nibble, words[:, :], 4 * j, 15, ALU.logical_shift_right, ALU.bitwise_and))
                deq_step(dve.tensor_tensor(wq[:, j, :], nibble, scale_bc[:, :], ALU.mult))
                deq_step(dve.tensor_tensor(wq[:, j, :], wq[:, j, :], zero_bc[:, :], ALU.subtract))

            def transpose_x(a, ja):
                wait(dve, x_in[ja], ring_count(a, ja, XR))
                wait(dve, ph_done, a - 1)
                dve.transpose(ring_a[:, ja % 2, :].rearrange("m (h q i) -> m q h i", h=MH, q=PH),
                              xt[:, ja, :].rearrange("c (h l q) -> c q h l", h=MH, q=PH)).then_inc(xT_ready, 1)

            transpose_x(0, 0)
            transpose_x(1, 1)
            dve.wait_ge(consts, N_CONSTS)
            pick_halves()
            dve.wait_ge(bg_in, 16)

            def step1(g, j):
                a, b = g - 1, g - 2
                ja, jb = (j - 1) % U, (j - 2) % U
                if isinstance(g, int) and g in (0, 2):
                    dve.wait_ge(ctx_in[g // 2], 16)
                if live(g, NG):
                    wait(dve, conv_done, g + 1)
                    wait(dve, tok_done, g - 1)
                    dve.tensor_tensor(hT[:, j % 2, :].rearrange("m (p s o) -> m s p o", p=PH, s=SUB),
                                      ps_conv[j % 2][:, :].rearrange("m (s p o) -> m s p o", s=SUB, p=PH),
                                      ctx_bc[:, bass.ds(g * P, P)].rearrange("m (s a o) -> m s a o", s=SUB, a=1).to_broadcast((P, SUB, PH, C)),
                                      ALU.add).then_inc(hT_ready, 1)
                if live(g + 2, NG):
                    transpose_x(g + 2, (j + 2) % U)
                if live(a, NG):
                    wait(dve, gate_done, a + 1)
                    dve.tensor_tensor(logit[:, :], ps_gate[:, 0:E], bg_bc[:, :], ALU.add).then_inc(logit_ready, 1)
                if live(b, NG):
                    wait(dve, rank_done, b + 1)
                    wait(dve, base_ready, b)
                    dve.tensor_tensor(rank[:, :], ps_rank[:, 0:E], base[:, :], ALU.add).then_inc(rank_ready, 1)
                if live(a, NG):
                    wait(dve, logit_ready, a + 1)
                if live(b, NG):
                    wait(dve, rank_ready, b + 1)
                    dve.tensor_tensor(base[:, :], base[:, :], ps_rank[:, E:2 * E], ALU.add).then_inc(base_ready, 1)
                if live(a, NG):
                    dve.max(top[:, :], logit[:, :]).then_inc(top_ready, 1)
                    wait(dve, top_ready, a + 1)
                if live(b, NG):
                    for k in range(2):
                        dve.scalar_tensor_tensor(picked[:, k, :], iota_e[:, :], expert_of[:, bass.ds(b, 1), k:k + 1].rearrange("p a k -> p (a k)"),
                                                 rank[:, :], ALU.is_equal, ALU.mult,
                                                 accum_out=row_of[:, bass.ds(b, 1), k:k + 1].rearrange("p a k -> p (a k)")).then_inc(row_ready, 1)
                if live(a, NG):
                    dve.max_index(topi[:, :], top[:, :], logit[:, :]).then_inc(topi_ready, 1)
                if live(b, NG):
                    wait(dve, row_ready, 2 * b + 2)
                    wait(dve, scattered[jb], (b - jb) * (32 // U))
                    dve.tensor_scalar(row_i[:, jb, :], row_of[:, bass.ds(b, 1), :].rearrange("p a k -> p (a k)"), 0.0, None, ALU.add).then_inc(rowi_ready, 1)
                if live(a, NG):
                    wait(dve, topi_ready, a + 1)
                    dve.tensor_scalar(expert_of[:, bass.ds(a, 1), :].rearrange("p a k -> p (a k)"), topi[:, 0:2], 0.0, None, ALU.add).then_inc(expert_ready, 1)
                    wait(dve, expert_ready, a + 1)
                    e1, e2 = (expert_of[:, bass.ds(a, 1), k:k + 1].rearrange("p a k -> p (a k)") for k in range(2))
                    dve.tensor_scalar(chosen1[:, :], iota_e[:, :], e1, None, ALU.is_equal).then_inc(chosen1_ready, 1)
                    wait(dve, chosen1_ready, a + 1)
                    wait(dve, rank_done, a - 3)
                    dve.scalar_tensor_tensor(chosen[:, ja, :], iota_e[:, :], e2, chosen1[:, :], ALU.is_equal, ALU.add).then_inc(chosen_ready, 1)

            stepped(dve, step1, 0, lo1, hi1, NG + 2)

            n = [0]

            def then(ins):
                n[0] += 1
                ins.then_inc(table, 1)
                dve.wait_ge(table, n[0])

            dve.wait_ge(base_ready, NG)
            then(dve.tensor_copy(tail_i[0:1, :], base[0:1, :]))
            then(dve.scalar_tensor_tensor(tcount[:, :], base[:, :], float(P - 1), region[:, :], ALU.add, ALU.subtract))
            then(dve.tensor_copy(tint[:, :], tcount[:, :]))
            then(dve.tensor_scalar(tshift[:, :], tint[:, :], 7, None, ALU.logical_shift_right))
            then(dve.tensor_copy(prefix[:, 0, E:], tshift[:, :]))
            for k in range(3):
                then(dve.tensor_tensor(prefix[:, k + 1, E:], prefix[:, k, E:], prefix[:, k, E - (1 << k):2 * E - (1 << k)], ALU.add))
            then(dve.tensor_tensor(tstart[:, :], prefix[:, 3, E:], prefix[:, 0, E:], ALU.subtract))
            then(dve.scalar_tensor_tensor(offs[:, :], tstart[:, :], float(-P), region[:, :], ALU.mult, ALU.add))
            then(dve.tensor_copy(doffs[:, 0:1], offs[:, 0:1]))
            then(dve.tensor_tensor(doffs[:, 1:E], offs[:, 1:E], offs[:, 0:E - 1], ALU.subtract))
            then(dve.tensor_scalar(used[:, :], prefix[:, 3, 2 * E - 1:2 * E], lane[:, 0:1], None, ALU.is_gt))
            then(dve.tensor_scalar(mask[:, :], tstart[:, :], lane[:, 0:1], None, ALU.is_le))
            then(dve.tensor_tensor(mprod[:, :], mask[:, :], doffs[:, :], ALU.mult))
            then(dve.tensor_reduce(tsum[:, 0:1], mprod[:, :], AX.X, ALU.add))
            then(dve.tensor_reduce(tsum[:, 1:2], mask[:, :], AX.X, ALU.add))
            then(dve.scalar_tensor_tensor(tsum[:, 2:3], lane[:, :], float(P), tsum[:, 0:1], ALU.mult, ALU.add))
            then(dve.tensor_scalar(tsum[:, 3:4], tsum[:, 1:2], -1.0, None, ALU.add))
            then(dve.tensor_scalar(tab_f[:, 0:2], tsum[:, 2:4], used[:, 0:1], None, ALU.mult))
            dve.sem_inc(tab_ready, 1)
            dve.wait_ge(tab_done, 1)
            dve.tensor_copy(tab[:, :], ps_misc[0:2, 256:256 + P]).then_inc(tab_ready, 1)

            dve.wait_ge(mlp_mm, 3)
            dve.tensor_tensor(att_n[:, :], ps_misc[:, 0:E], b2_bc[:, :], ALU.add).then_inc(mlp_ev, 1)
            dve.wait_ge(mlp_ev, 3)
            dve.tensor_reduce(att_m[:, :], att_n[:, :], AX.X, ALU.max).then_inc(mlp_ev, 1)
            dve.wait_ge(mlp_ev, 4)
            dve.tensor_scalar(att[:, :], att_n[:, :], att_m[:, 0:1], None, ALU.subtract).then_inc(mlp_ev, 1)
            dve.wait_ge(mlp_ev, 6)
            dve.reciprocal(att_r[:, :], att_s[:, :]).then_inc(mlp_ev, 1)
            dve.wait_ge(mlp_ev, 7)
            dve.tensor_scalar(att_n[:, :], att_x[:, :], att_r[:, 0:1], None, ALU.mult).then_inc(mlp_ev, 1)
            dve.wait_ge(mlp_mm, 4)
            dve.tensor_copy(attT[:, :], ps_misc[0:E, 0:N]).then_inc(mlp_ev, 1)
            for k in range(2):
                dve.wait_ge(mlp_mm, 5 + k)
                src = ps_mix[k][:, :].rearrange("n (o i) -> n i o", i=C)
                ins = dve.tensor_copy(mix_sb[:, :, k * 16:k * 16 + 16], src)
                if k == 0:
                    ins.then_inc(mlp_ev, 1)
                    dve.wait_ge(mlp_mm, 7)
                    dve.tensor_copy(mixb_sb[:, :], ps_misc[:, 0:C])
                else:
                    ins.then_inc(mlp_ev, 1)

            def find_places(first, last):
                rows2 = row_of[:, :, :].rearrange("p g k -> p (g k)")
                expert2 = expert_of[:, :, :].rearrange("p g k -> p (g k)")
                for e in range(first, last):
                    if e == 0:
                        then(dve.tensor_scalar(shift_s[:, :], expert2, 0.0, offs[:, 0:1], ALU.is_equal, ALU.mult))
                    else:
                        then(dve.tensor_scalar(shift_e[:, :], expert2, float(e), offs[:, e:e + 1], ALU.is_equal, ALU.mult))
                        then(dve.tensor_tensor(shift_s[:, :], shift_s[:, :], shift_e[:, :], ALU.add))
                if last == E:
                    dve.tensor_tensor(place_i[:, :, :].rearrange("p g k -> p (g k)"), rows2, shift_s[:, :], ALU.subtract).then_inc(place_ready, 1)

            dve.wait_ge(be_in, 16)
            dve.wait_ge(tail_out, 16 * E)

            def step2(s, j):
                a = s + 1
                if live(a, NT):
                    ja = (j + 1) % U
                    wait(dve, list_in[ja], (a - ja) * (64 // U) + 64)
                    wait(dve, exp_done, a - 1)
                    dve.transpose(hT[:, ja % 2, :].rearrange("m (p h r) -> m h p r", p=PH, h=MH),
                                  htok[:, ja, :].rearrange("r (h p l) -> r h p l", h=MH, p=PH)).then_inc(lT_ready, 1)
                if live(s, NT):
                    expert = dve.value_load(tab[1:2, bass.ds(s, 1)], min_val=0, max_val=E - 1)
                    wait(dve, exp_done, s + 1)
                    wait(dve, result_ready, s - 1)
                    dve.tensor_tensor(ring_a[:, j % 2, :], ps_exp[j % 2][:, :],
                                      be_bc[:, bass.ds(expert, 1), :].rearrange("p a n -> p (a n)"), ALU.add).then_inc(sum_ready, 1)
                if isinstance(s, int) and 1 <= s < 5:
                    dequantize(s - 1)
                if isinstance(s, int) and 5 <= s < 7:
                    find_places((s - 5) * E // 2, (s - 4) * E // 2)

            stepped(dve, step2, -1, lo2, hi2, NT)
            assert deqs[0] == N_DEQ
            dve.wait_ge(mix_in, 16 * (1 + SUB))

            def step3(g, j):
                a = g + 2
                if live(a, NG):
                    ja = (j + 2) % U
                    wait(dve, x3_in[ja], ring_count(a, ja, XR))
                    wait(dve, gathered[ja % 2], (a - ja % 2) * 16 + 32)
                    wait(dve, mixed_done, a - 1)
                    wait(dve, yb_ready, a - 1)
                    dve.tensor_tensor(ring_a[:, ja % 2, :], xt[:, ja, :], htok[:, 2 * (ja % 2), :], ALU.add).then_inc(ya_ready, 1)
                b = g + 1
                if live(b, NG):
                    jb = (j + 1) % U
                    wait(dve, mixed_done, b + 1)
                    wait(dve, lin_done, b - 1)
                    dve.tensor_tensor(hT[:, jb % 2, :].rearrange("l (j t) -> l j t", j=4),
                                      ps_mix[jb % 2][:, :].rearrange("l (j t) -> l j t", j=4),
                                      mixb_bc[:, bass.ds(b * P, P)].rearrange("l (a t) -> l a t", a=1).to_broadcast((P, 4, P)),
                                      ALU.add).then_inc(mixed_ready, 1)
                if live(a, NG):
                    wait(dve, ya_ready, a + 1)
                    dve.tensor_tensor(ring_a[:, ja % 2, :], ring_a[:, ja % 2, :], htok[:, 2 * (ja % 2) + 1, :], ALU.add).then_inc(y_ready, 1)
                if live(g, NG):
                    wait(dve, lin_done, g + 1)
                    wait(dve, yb_ready, g + 1)
                    wait(dve, out_out[j % 2], (g - j % 2) * 8)
                    dve.tensor_tensor(orow[:, j % 2, :], ps_lin[j % 2][:, :], ring_b[:, j % 2, :], ALU.add).then_inc(out_ready, 1)

            stepped(dve, step3, -2, lo1, hi1, NG)

        @block.tensor
        def _(pe):
            pe.wait_ge(ident_ready, 2)
            pe.wait_ge(cond_in, 32)
            pe.transpose(ps_misc[:, 0:N], cond_sb[:, :], ident[:, :]).then_inc(condT_done, 1)
            pe.transpose(ps_misc[:, N:N + C], cw_sb[:, :], ident[0:C, 0:C]).then_inc(condT_done, 1)
            pe.wait_ge(condT_ready, 2)
            pe.matmul(ps_misc[:, 0:C], condT[:, :], cwT[:, :], start=True, stop=True).then_inc(ctx_mm, 1)
            pe.wait_ge(wsel_ready, 1)
            for s in range(SHIFTS):
                for p in range(PH):
                    at = (s * PH + p) * C
                    mm = pe.transpose(bank[6][:, at:at + C],
                                      wsel[:, s * PH + p, :, :].rearrange("o q i -> o (q i)"), ident[0:C, 0:C])
            mm.then_inc(wT_done, 1)

            def step1(g, j):
                if live(g, NG):
                    wait(pe, ph_ready, g + 1)
                    wait(pe, hT_ready, g - 1)
                    if isinstance(g, int) and g == 0:
                        pe.wait_ge(wconv_ready, 1)
                    for s in range(SUB):
                        for t in range(SHIFTS):
                            mm = pe.matmul(ps_conv[j % 2][:, s * P:(s + 1) * P], phases[:, j % 2, s, t:t + P],
                                           wconv[:, t, :, :].rearrange("k p o -> k (p o)"),
                                           start=(t == 0), stop=(t == SHIFTS - 1))
                    mm.then_inc(conv_done, 1)
                a = g + 1
                if live(a, NG):
                    wait(pe, xT_ready, a + 1)
                    wait(pe, ph_ready, a)
                    for h in range(MH):
                        mm = pe.transpose(ps_ph[:, h * P:(h + 1) * P], ring_a[:, (j + 1) % 2, h * P:(h + 1) * P], ident[:, :])
                    mm.then_inc(ph_done, 1)
                a = g - 1
                if live(a, NG):
                    ja = (j - 1) % U
                    wait(pe, hT_ready, a + 1)
                    wait(pe, logit_ready, a)
                    if isinstance(a, int) and a == 0:
                        pe.wait_ge(gate_in, 16)
                        pe.wait_ge(consts, N_CONSTS)
                    for p in range(PH):
                        mm = pe.matmul(ps_gate[:, 0:P], hT[:, ja % 2, p * P:(p + 1) * P], wg[:, p, :],
                                       start=(p == 0), stop=(p == PH - 1))
                    mm.then_inc(gate_done, 1)
                    wait(pe, tok_ready, a)
                    for p in range(PH):
                        mm = pe.transpose(ps_tok[:, p * P:(p + 1) * P], hT[:, ja % 2, p * P:(p + 1) * P], ident[:, :])
                    mm.then_inc(tok_done, 1)
                a = g - 2
                if live(a, NG):
                    ja = (j - 2) % U
                    wait(pe, chosen_ready, a + 1)
                    wait(pe, base_ready, a)
                    pe.matmul(ps_rank[:, 0:E], before[:, :], chosen[:, ja, :], start=True, stop=True)
                    pe.matmul(ps_rank[:, E:2 * E], ones[:, :], chosen[:, ja, :], start=True, stop=True).then_inc(rank_done, 1)

            stepped(pe, step1, -1, lo1, hi1, NG + 2)

            pe.wait_ge(mlp_in, 16 * 8)
            pe.matmul(ps_misc[:, 0:N], w0_sb[:, :], condT[:, :], start=True, stop=True).then_inc(mlp_mm, 1)
            pe.wait_ge(mlp_ev, 1)
            pe.matmul(ps_misc[:, 0:N], w1_sb[:, :], g0[:, :], start=True, stop=True).then_inc(mlp_mm, 1)
            pe.wait_ge(mlp_ev, 2)
            pe.wait_ge(tab_ready, 1)
            pe.transpose(ps_misc[0:2, 256:256 + P], tab_f[:, :], ident[:, :]).then_inc(tab_done, 1)
            pe.wait_ge(tab_ready, 2)
            pe.matmul(ps_misc[:, 0:E], g1[:, :], w2_sb[:, :], start=True, stop=True).then_inc(mlp_mm, 1)
            pe.wait_ge(mlp_ev, 8)
            pe.transpose(ps_misc[0:E, 0:N], att_n[:, :], ident[:, :]).then_inc(mlp_mm, 1)
            pe.wait_ge(mlp_ev, 9)
            for k in range(2):
                pe.matmul(ps_mix[k][:, :], attT[:, :], mixw_sb[:, k * 512:(k + 1) * 512], start=True, stop=True).then_inc(mlp_mm, 1)
            pe.matmul(ps_misc[:, 0:C], attT[:, :], mixb_w[:, :], start=True, stop=True).then_inc(mlp_mm, 1)
            pe.wait_ge(we_in, 16 * E)

            def step2(s, j):
                if live(s, NT):
                    expert = pe.value_load(tab[1:2, bass.ds(s, 1)], min_val=0, max_val=E - 1)
                    wait(pe, lT_ready, s + 1)
                    wait(pe, sum_ready, s - 1)
                    for p in range(PH):
                        mm = pe.matmul(ps_exp[j % 2][:, :], hT[:, j % 2, p * P:(p + 1) * P],
                                       we[:, bass.ds(expert, 1), p, :].rearrange("m a n -> m (a n)"),
                                       start=(p == 0), stop=(p == PH - 1))
                    mm.then_inc(exp_done, 1)

            stepped(pe, step2, 0, lo2, hi2, NT)
            pe.wait_ge(mix_in, 16 * (1 + SUB))
            pe.wait_ge(deq, N_DEQ)

            def step3(g, j):
                a = g + 1
                if live(a, NG):
                    ja = (j + 1) % 2
                    wait(pe, y_ready, a + 1)
                    wait(pe, mixed_ready, a - 1)
                    for q in range(4):
                        cols = ring_a[:, ja, q:L:4]
                        mm = pe.matmul(ps_mix[ja][:, q * P:(q + 1) * P], cols,
                                       mix_bd[:, bass.ds(a, 1), :].rearrange("c a t -> c (a t)"), start=True, stop=True)
                    mm.then_inc(mixed_done, 1)
                if live(g, NG):
                    wait(pe, mixed_ready, g + 1)
                    wait(pe, out_ready, g - 1)
                    for q in range(4):
                        mm = pe.matmul(ps_lin[j % 2][:, :], hT[:, j % 2, q * P:(q + 1) * P], wq[:, q, :],
                                       start=(q == 0), stop=(q == 3))
                    mm.then_inc(lin_done, 1)

            stepped(pe, step3, -1, lo1, hi1, NG)


_INS = ['x', 'cond_128', 'fside_S_0', 'L0_cond_weight', 'L0_cond_c_weight', 'L0_ffn_W_gate', 'L0_ffn_b_gate',
        'L0_ffn_W_e', 'L0_ffn_b_e', 'L1_cond_W0', 'L1_cond_b0', 'L1_cond_W1', 'L1_cond_b1', 'L1_cond_W2',
        'L1_cond_b2', 'L1_cond_weight', 'L1_cond_bias_k', 'L1_ffn_qweight', 'L1_ffn_scales', 'L1_ffn_zeros',
        'L1_ffn_bias']


def kernel(**inputs):
    import concourse.bacc as bacc
    from concourse.bass_utils import run_bass_kernel_spmd

    nc = bacc.Bacc("TRN2", target_bir_lowering=False, num_devices=1)
    arrays, args = {}, []
    for name in _INS:
        a = np.ascontiguousarray(inputs[name])
        arrays[f"in_{name}"] = a
        args.append(nc.dram_tensor(f"in_{name}", a.shape, mybir.dt.from_np(a.dtype), kind="ExternalInput").ap())
    result = nc.dram_tensor("out", (N, C, L), F32, kind="ExternalOutput").ap()
    build_program(nc, *args, result)
    r = run_bass_kernel_spmd(nc, [arrays], core_ids=[0])
    return r.results[0]["out"]
```

```python
from contextlib import ExitStack

import numpy as np

import concourse.bass as bass
from concourse import mybir

F32 = mybir.dt.float32
BF16 = mybir.dt.bfloat16
F32R = mybir.dt.float32r
I32 = mybir.dt.int32
U32 = mybir.dt.uint32
ALU = mybir.AluOpType
ACT = mybir.ActivationFunctionType
AX = mybir.AxisListType

P = 128
N, C, L = 128, 32, 512
SUB = P // C
NG = N // SUB
TAPS, PAD, CG = 9, 4, 8
PH = L // P
B = 32
MH = P // B
SHIFTS = 3
KW = TAPS + 2 * (PH - 1)
E = 8
REGION = P + N * C
NT = (2 * N * C - E) // P + E
SURE = 2 * N * C // P
U = 4
XR = 4
RK = 2 * B


def live(i, n):
    return not isinstance(i, int) or 0 <= i < n


def wait(eng, sem, value):
    if not isinstance(value, int) or value > 0:
        eng.wait_ge(sem, value)


def stepped(eng, step, first, lo, hi, last):
    assert (hi - lo) % U == 0 and lo % U == 0
    for i in range(first, lo):
        step(i, i % U)
    with eng.Fori(0, (hi - lo) // U) as k:
        base = k * U + lo
        for j in range(U):
            step(base + j, j)
    for i in range(hi, last):
        step(i, i % U)


def ring_count(i, j, ring):
    return (i - j % ring) * (16 // ring) + 16


def build_program(nc, x, cond, fside, conv_w, ctx_w, w_gate, b_gate, w_e, b_e,
                  w0, b0, w1, b1, w2, b2, mix_w, mix_b, qweight, scales, zeros, bias, out):
    ctx = ExitStack()
    with ctx:
        def sb(name, shape, dt=F32):
            return ctx.enter_context(nc.sbuf_tensor(name, shape, dt))

        def sem(name):
            return ctx.enter_context(nc.semaphore(name))

        def dram(name, shape):
            return nc.dram_tensor(name, shape, F32, kind="Internal").ap()

        lists_d = dram("lists_d", (E * REGION, L))
        result_d = dram("result_d", (NT * P, L))
        ctx_d = dram("ctx_d", (N, C))
        mixb_d = dram("mixb_d", (N, C))
        mix_d = dram("mix_d", (N, C, C))

        x_g = x.rearrange("(g s) c l -> g (s c) l", s=SUB)
        out_g = out.rearrange("(g s) c l -> g (s c) l", s=SUB)

        we = sb("we", [P, E, PH, L])
        be_bc = sb("be_bc", [P, E, L])
        ctx_bc = sb("ctx_bc", [P, N * C])
        mixb_row = ctx_bc[0:2, :]
        mix_bd = sb("mix_bd", [P, NG, P])
        wq = sb("wq", [P, 4, L], F32R)
        scale_bc = sb("scale_bc", [P, L])
        zero_bc = sb("zero_bc", [P, L])
        bias_bc = sb("bias_bc", [P, L])
        xt = sb("xt", [P, XR, L])
        ring_a = sb("ring_a", [P, 2, L])
        phases = sb("phases", [P, 2, SUB, P + 2])
        hT = sb("hT", [P, 2, L])
        htok = sb("htok", [P, U, L])
        ring_b = sb("ring_b", [P, U, L])
        orow = sb("orow", [P, 2, L])
        ident = sb("ident", [P, P])
        before = sb("before", [P, P], BF16)
        ones = sb("ones", [P, P], BF16)
        wconv = sb("wconv", [P, SHIFTS, PH, C])
        wfull = sb("wfull", [C, C, KW])
        wg = sb("wg", [P, PH, P])
        bg_bc = sb("bg_bc", [P, E])
        iota_e = sb("iota_e", [P, E])
        region = sb("region", [P, E])
        lane = sb("lane", [P, 1])
        base = sb("base", [P, E])
        logit = sb("logit", [P, E])
        top = sb("top", [P, E])
        topi = sb("topi", [P, E], U32)
        chosen1 = sb("chosen1", [P, E])
        chosen = sb("chosen", [P, U, E], BF16)
        rank = sb("rank", [P, E])
        picked = sb("picked", [P, 2, E])
        expert_of = sb("expert_of", [P, NG, 2])
        row_of = sb("row_of", [P, NG, 2])
        row_i = sb("row_i", [P, U, 2], I32)
        tint = sb("tint", [P, E], I32)
        tshift = sb("tshift", [P, E], I32)
        prefix = sb("prefix", [P, 4, 2 * E])
        tstart = sb("tstart", [P, E])
        offs = sb("offs", [P, E])
        doffs = sb("doffs", [P, E])
        mask = sb("mask", [P, E])
        mprod = sb("mprod", [P, E])
        tsum = sb("tsum", [P, 4])
        used = sb("used", [P, 1])
        tab_f = sb("tab_f", [P, 3])
        tab = sb("tab", [3, P], I32)
        shift_e = sb("shift_e", [P, NG * 2])
        shift_s = sb("shift_s", [P, NG * 2])
        place_i = sb("place_i", [P, NG, 2], I32)
        gidx = sb("gidx", [P, U, 2], I32)
        cond_sb = sb("cond_sb", [N, P])
        condT = sb("condT", [P, N])
        cw_sb = sb("cw_sb", [C, P])
        cwT = sb("cwT", [P, C])
        fs_bc = sb("fs_bc", [P, C])
        ctx_sb = sb("ctx_sb", [N, C])
        w0_sb = sb("w0_sb", [P, P])
        w1_sb = sb("w1_sb", [P, P])
        w2_sb = sb("w2_sb", [P, E])
        b0_sb = sb("b0_sb", [P, 1])
        b1_sb = sb("b1_sb", [P, 1])
        b2_bc = sb("b2_bc", [P, E])
        mixb_w = sb("mixb_w", [E, C])
        g0 = sb("g0", [P, N])
        g1 = sb("g1", [P, N])
        att = sb("att", [N, E])
        att_m = sb("att_m", [N, 1])
        att_x = sb("att_x", [N, E])
        att_s = sb("att_s", [N, 1])
        att_r = sb("att_r", [N, 1])
        att_n = sb("att_n", [N, E])
        attT = sb("attT", [E, N])
        mixb_sb = sb("mixb_sb", [N, C])
        mixw_sb = ring_b[0:E, 0:2, :].rearrange("k h n -> k (h n)")
        mix_sb = sb("mix_sb", [N, C, C])
        wsel = htok[0:C, 1:4, :].rearrange("o a (b q i) -> o (a b) q i", q=PH, i=C)
        words = sb("words", [P, L], I32)
        y_t = we[:, 0, :, :]
        part = we[:, 1, :, :]
        found = we[:, 2:4, :, :].rearrange("p e q n -> p (e q) n").rearrange("p (g k) n -> p g k n", k=2)
        high = sb("high", [P, 2, L], F32R)
        low = sb("low", [P, 2, L], F32R)
        cls = sb("cls", [P, P])
        is_sum = sb("is_sum", [P, P])
        sel_b = sb("sel_b", [2, P])
        ones_r = sb("ones_r", [P, RK], F32R)
        cls_i = sb("cls_i", [P, 1], I32)
        cls_p = sb("cls_p", [P, 1])
        term = sb("term", [P, 3])
        ysum = sb("ysum", [P, 2])
        ysum_cols = sb("ysum_cols", [P, 2, P])
        terms_t = sb("terms_t", [RK, 2, P], F32R)
        terms_w = sb("terms_w", [RK, L], F32R)
        lane_i = sb("lane_i", [P, 1], I32)
        odd_i = sb("odd_i", [P, 1], I32)
        odd = sb("odd", [P, 1])
        even = sb("even", [P, 1])

        bank = [ctx.enter_context(nc.psum_tensor(f"bank{i}", [P, 512], F32)) for i in range(8)]
        ps_ph, ps_conv, ps_tok, ps_gate, ps_rank, ps_misc = (
            bank[1], bank[2:4], bank[4], bank[5], bank[6], bank[7])
        ps_exp = bank[2:4]
        ps_w = bank[4:7]
        ps_kernels = bank[0:2]
        ps_mix, ps_lin, ps_terms, ps_low = bank[4:6], bank[2:4], bank[6:8], bank[0:2]

        ident_ready = sem("ident_ready")
        pads_ready = sem("pads_ready")
        consts = sem("consts")
        mixbd_zero = sem("mixbd_zero")
        mixb_one = sem("mixb_one")
        wfull_zero = sem("wfull_zero")
        convw_in = sem("convw_in")
        cond_in = sem("cond_in")
        fs_in = sem("fs_in")
        gate_in = sem("gate_in")
        bg_in = sem("bg_in")
        mlp_in = sem("mlp_in")
        q_in = sem("q_in")
        be_in = sem("be_in")
        we_in = sem("we_in")
        x_in = [sem(f"x_in{i}") for i in range(XR)]
        dve_taps = sem("dve_taps")
        act_taps = sem("act_taps")
        wT_done = sem("wT_done")
        wconv_ready = sem("wconv_ready")
        condT_done = sem("condT_done")
        condT_ready = sem("condT_ready")
        ctx_mm = sem("ctx_mm")
        ctx_ready = sem("ctx_ready")
        ctx_out = sem("ctx_out")
        ctx_in = [sem(f"ctx_in{i}") for i in range(2)]
        deq = sem("deq")
        xT_ready = sem("xT_ready")
        ph_done = sem("ph_done")
        ph_ready = sem("ph_ready")
        conv_done = sem("conv_done")
        hT_ready = sem("hT_ready")
        gate_done = sem("gate_done")
        tok_done = sem("tok_done")
        tok_ready = sem("tok_ready")
        logit_ready = sem("logit_ready")
        top_ready = sem("top_ready")
        topi_ready = sem("topi_ready")
        expert_ready = sem("expert_ready")
        chosen1_ready = sem("chosen1_ready")
        chosen_ready = sem("chosen_ready")
        rank_done = sem("rank_done")
        rank_ready = sem("rank_ready")
        base_ready = sem("base_ready")
        row_ready = sem("row_ready")
        rowi_ready = sem("rowi_ready")
        scatter_go = sem("scatter_go")
        scattered = [sem(f"scattered{i}") for i in range(U)]
        table = sem("table")
        tab_done = sem("tab_done")
        tab_ready = sem("tab_ready")
        head_out = sem("head_out")
        place_ready = sem("place_ready")
        mlp_mm = sem("mlp_mm")
        mlp_ev = sem("mlp_ev")
        mix_out = sem("mix_out")
        mix_in = sem("mix_in")
        list_in = [sem(f"list_in{i}") for i in range(U)]
        lT_ready = sem("lT_ready")
        exp_done = sem("exp_done")
        sum_ready = sem("sum_ready")
        result_ready = sem("result_ready")
        result_out = [sem(f"result_out{i}") for i in range(U)]
        gidx_ready = sem("gidx_ready")
        gather_go = sem("gather_go")
        gathered = [sem(f"gathered{i}") for i in range(U)]
        x3_in = [sem(f"x3_in{i}") for i in range(XR)]
        ya_ready = sem("ya_ready")
        y_ready = sem("y_ready")
        ysum_ready = sem("ysum_ready")
        mixed_done = sem("mixed_done")
        terms_done = sem("terms_done")
        high_ready = sem("high_ready")
        thigh_ready = sem("thigh_ready")
        low_ready = sem("low_ready")
        tlow_ready = sem("tlow_ready")
        lin_done = sem("lin_done")
        low_done = sem("low_done")
        colsum_done = sem("colsum_done")
        scaled_ready = sem("scaled_ready")
        part_ready = sem("part_ready")
        out_ready = sem("out_ready")
        out_out = [sem(f"out_out{i}") for i in range(2)]

        N_CONSTS = 12
        WARM_START, WARM, WARM_END = 8, 34, 42
        N_NIBBLES = 7 + 4 * 2
        N_DEQ = N_NIBBLES + 3 + 3 + 3 + 9
        CTX_FIRST = 2 * P
        zeros_t = orow[:, 0, :]
        lo1, hi1 = U, NG - 2 * U
        lo3, hi3 = U, NG - U
        lo2, hi2 = 2 * U, NT // U * U - 2 * U

        block = ctx.enter_context(nc.Block())

        def pick_taps(copy, phases_of, taps_ready):
            for t in range(SHIFTS):
                for p in phases_of:
                    k0 = PH * t - p + PH - 1
                    ins = copy(wsel[:, t * PH + p, :, :], wfull[:, :, k0:k0 + PH].rearrange("o i q -> o q i"))
                ins.then_inc(taps_ready, 1)

        @block.sync
        def _(sp):
            sp.dma_start(cond_sb[:, :], cond).then_inc(cond_in, 16)
            sp.dma_start(cw_sb[:, :], ctx_w).then_inc(cond_in, 16)
            sp.wait_ge(wfull_zero, 1)
            for s in range(C // CG):
                rows = slice(s * CG, (s + 1) * CG)
                sp.dma_start(wfull[rows, rows, PH - 1:PH - 1 + TAPS], conv_w[rows]).then_inc(convw_in, 16)
            for g in range(XR):
                sp.dma_start(xt[:, g, :], x_g[g]).then_inc(x_in[g], 16)
            sp.wait_ge(ctx_ready, 1)
            sp.dma_start(ctx_d, ctx_sb[:, :]).then_inc(ctx_out, 16)
            sp.wait_ge(ctx_out, 16)
            ctx_row = ctx_d.rearrange("(a n) c -> a (n c)", a=1)
            for i, cols in enumerate((slice(0, CTX_FIRST), slice(CTX_FIRST, N * C))):
                sp.dma_start(ctx_bc[:, cols], ctx_row[:, cols].to_broadcast((P, cols.stop - cols.start))).then_inc(ctx_in[i], 16)

            def load_we(e):
                return sp.dma_start(we[:, bass.ds(e, 1), :, :].rearrange("m a p n -> m (a p n)"),
                                    w_e[bass.ds(e, 1)].rearrange("a (m p) n -> m (a p n)", p=PH)).then_inc(we_in, 16)

            def zero_head(e):
                return sp.dma_start(lists_d[bass.ds(e * REGION, P), :], zeros_t).then_inc(head_out, 16)

            sp.wait_ge(consts, N_CONSTS)
            load_we(0)
            zero_head(0)
            with sp.Fori(0, NG // XR - 1) as k:
                for j in range(XR):
                    sp.wait_ge(xT_ready, k * XR + j + 1)
                    sp.dma_start(xt[:, j, :], x_g[bass.ds(k * XR + XR + j, 1)].rearrange("a p l -> p (a l)")).then_inc(x_in[j], 16)
                load_we(k + 1)
                zero_head(k + 1)

            sp.wait_ge(head_out, 16 * E)
            for s in scattered:
                sp.wait_ge(s, 32 * (NG // U))
            sp.wait_ge(tab_ready, 2)
            row_reg = sp.alloc_register("row_reg")

            def list_step(s, j):
                a = s + 3
                if live(a, NT):
                    ja = (j + 3) % U
                    sp.reg_load(row_reg, tab[0:1, bass.ds(a, 1)])
                    row = sp.snap(row_reg, min_val=0, max_val=E * REGION - P)
                    wait(sp, lT_ready, a - 3)
                    for mh in range(MH):
                        sp.dma_start(htok[mh * B:(mh + 1) * B, ja, :].rearrange("r (h n) -> r h n", h=MH),
                                     lists_d[bass.ds(row, P), mh * P:(mh + 1) * P].rearrange("(h r) n -> r h n", r=B)
                                     ).then_inc(list_in[ja], 16)

            stepped(sp, list_step, -3, lo2, hi2 - U, NT - 3)

            def row_step(g, j):
                a = g + 6
                if live(a, NG):
                    ja = (j + 6) % U
                    wait(sp, ya_ready, a - 3)
                    sp.dma_start(xt[:, ja, :], x_g[bass.ds(a, 1)].rearrange("a p l -> p (a l)")).then_inc(x3_in[ja], 16)
                if live(g, NG):
                    wait(sp, out_ready, g + 1)
                    sp.dma_start(out_g[bass.ds(g, 1)].rearrange("a p l -> p (a l)"), orow[:, j % 2, :]).then_inc(out_out[j % 2], 16)

            stepped(sp, row_step, -6, lo3, hi3 - U, NG)
            for s in out_out:
                sp.wait_ge(s, 16 * (NG // 2))

        @block.gpsimd
        def _(pool):
            pool.memset(ident[:, :], 0.0).then_inc(ident_ready, 1)
            pool.wait_ge(ident_ready, 1)
            pool.affine_select(out=ident[:, :], in_=ident[:, :], compare_op=ALU.not_equal, fill=1.0, base=0,
                               pattern=[[-1, P]], channel_multiplier=1).then_inc(ident_ready, 1)
            for edge in (0, P + 1):
                pool.memset(phases[:, :, :, edge:edge + 1], 0.0).then_inc(pads_ready, 1)
            pool.memset(wg[:, :, :], 0.0).then_inc(consts, 1)
            pool.memset(before[:, :], 1.0).then_inc(consts, 1)
            pool.wait_ge(consts, 2)
            pool.dma_start(wg[:, :, 0:E], w_gate.rearrange("(m p) e -> m p e", p=PH)).then_inc(gate_in, 16)
            pool.affine_select(out=before[:, :], in_=before[:, :], compare_op=ALU.is_ge, fill=0.0, base=-1,
                               pattern=[[1, P]], channel_multiplier=-1).then_inc(consts, 1)
            pool.memset(ones[:, :], 1.0).then_inc(consts, 1)
            exact = dict(allow_small_or_imprecise_dtypes=True)
            pool.iota(iota_e[:, :], pattern=[[1, E]], base=0, channel_multiplier=0, **exact).then_inc(consts, 1)
            pool.iota(region[:, :], pattern=[[REGION, E]], base=P, channel_multiplier=0, **exact).then_inc(consts, 1)
            pool.iota(base[:, :], pattern=[[REGION, E]], base=P, channel_multiplier=0, **exact).then_inc(consts, 1)
            pool.iota(lane[:, :], pattern=[[0, 1]], base=0, channel_multiplier=1, **exact).then_inc(consts, 1)
            pool.iota(lane_i[:, :], pattern=[[0, 1]], base=0, channel_multiplier=1).then_inc(consts, 1)
            pool.iota(cls[:, :], pattern=[[0, P // B], [1, B // 2], [0, 2]], base=0, channel_multiplier=0, **exact).then_inc(consts, 1)
            pool.memset(prefix[:, :, :], 0.0).then_inc(consts, 1)
            pool.memset(zeros_t, 0.0).then_inc(consts, 1)
            for dst, src in ((w0_sb[:, :], w0), (w1_sb[:, :], w1), (w2_sb[:, :], w2),
                             (b0_sb[:, :], b0.rearrange("(n a) -> n a", a=1)),
                             (b1_sb[:, :], b1.rearrange("(n a) -> n a", a=1)),
                             (b2_bc[:, :], b2.rearrange("(a e) -> a e", a=1).to_broadcast((P, E))),
                             (mixw_sb, mix_w.rearrange("k o i a -> k (o i a)")),
                             (mixb_w[:, :], mix_b)):
                pool.dma_start(dst, src).then_inc(mlp_in, 16)
            pool.memset(mix_bd[:, :, :], 0.0).then_inc(mixbd_zero, 1)

            def scatter_step(g, j):
                wait(pool, tok_ready, g + 1)
                wait(pool, rowi_ready, g + 1)
                pool.sem_inc(scatter_go, 1)
                for k in range(2):
                    pool.indirect_dma_start(lists_d, bass.IndirectOffsetOnAxis(ap=row_i[:, j, k:k + 1], axis=0),
                                            htok[:, j, :], None, bounds_check=E * REGION - 1,
                                            oob_is_err=False).then_inc(scattered[j], 16)

            stepped(pool, scatter_step, 0, lo1, hi1, NG)

            pool.memset(mixb_row, 1.0).then_inc(mixb_one, 1)

            for i, s in enumerate(result_out):
                pool.wait_ge(s, 16 * len(range(i, NT, U)))

            def gather(g, j):
                wait(pool, gidx_ready, g + 1)
                wait(pool, y_ready, g - 3)
                pool.sem_inc(gather_go, 1)
                for k in range(2):
                    pool.indirect_dma_start(found[:, j, k, :], None, result_d,
                                            bass.IndirectOffsetOnAxis(ap=gidx[:, j, k:k + 1], axis=0),
                                            bounds_check=NT * P - 1, oob_is_err=False).then_inc(gathered[j], 16)

            def step3(g, j):
                if live(g + 4, NG):
                    gather(g + 4, (j + 4) % U)
                a = g - 1
                if live(a, NG):
                    ja = (j - 1) % U
                    wait(pool, part_ready, a + 1)
                    wait(pool, out_out[ja % 2], (a - ja % 2) * 8)
                    pool.tensor_tensor(orow[:, ja % 2, :], part[:, ja, :], y_t[:, ja, :], ALU.add).then_inc(out_ready, 1)

            stepped(pool, step3, -4, lo3, hi3 - U, NG + 1)

        @block.scalar
        def _(act):
            act.dma_start(fs_bc[:, :], fside.rearrange("(a c) -> a c", a=1).to_broadcast((P, C))).then_inc(fs_in, 16)
            act.wait_ge(ident_ready, 2)
            act.copy(g0[:, 0:1], ident[:, 0:1])
            act.wait_ge(convw_in, 16 * (C // CG))
            pick_taps(act.copy, range(PH // 2, PH), act_taps)

            def step1(g, j):
                a = g + 1
                if live(a, NG):
                    wait(act, ph_done, a + 1)
                    wait(act, conv_done, a - 1)
                    act.copy(phases[:, (j + 1) % 2, :, 1:P + 1].rearrange("k s (h l) -> k h s l", h=MH),
                             ps_ph[:, :].rearrange("k (h s l) -> k h s l", h=MH, s=SUB)).then_inc(ph_ready, 1)
                a = g - 1
                if live(a, NG):
                    ja = (j - 1) % U
                    wait(act, tok_done, a + 1)
                    wait(act, scattered[ja], (a - ja) * (32 // U))
                    act.copy(htok[:, ja, :].rearrange("t (h p l) -> t p h l", h=MH, p=PH),
                             ps_tok[:, :].rearrange("t (p h l) -> t p h l", p=PH, h=MH)).then_inc(tok_ready, 1)

                if isinstance(g, int) and g == -1:
                    act.dma_start(bg_bc[:, :], b_gate.rearrange("(a e) -> a e", a=1).to_broadcast((P, E))).then_inc(bg_in, 16)
                    for u in range(2):
                        act.dma_start(words[u:P:2, :], qweight).then_inc(q_in, 16)
                    act.dma_start(scale_bc[:, :], scales.rearrange("n a -> a n").to_broadcast((P, L))).then_inc(q_in, 16)
                    act.dma_start(zero_bc[:, :], zeros.rearrange("n a -> a n").to_broadcast((P, L))).then_inc(q_in, 16)
                    act.dma_start(bias_bc[:, :], bias.rearrange("(a n) -> a n", a=1).to_broadcast((P, L))).then_inc(q_in, 16)
                if isinstance(g, int) and g == lo1 - 1:
                    act.dma_start(be_bc[:, :, :].rearrange("p e n -> p (e n)"),
                                  b_e.rearrange("(a e) n -> a (e n)", a=1).to_broadcast((P, E * L))).then_inc(be_in, 16)
                if isinstance(g, int) and g >= hi1:
                    if g == hi1:
                        act.wait_ge(mlp_in, 16 * 8)
                        act.wait_ge(mlp_mm, 1)
                        act.activation(g0[:, :], ps_misc[:, 0:N], ACT.Gelu, bias=b0_sb[:, 0:1]).then_inc(mlp_ev, 1)
                    if g == hi1 + 1:
                        act.wait_ge(mlp_mm, 2)
                        act.activation(g1[:, :], ps_misc[:, 0:N], ACT.Gelu, bias=b1_sb[:, 0:1]).then_inc(mlp_ev, 1)
                    if g == hi1 + 3:
                        act.wait_ge(mlp_ev, 5)
                        act.activation(att_x[:, :], att[:, :], ACT.Exp, accum_out=att_s[:, 0:1]).then_inc(mlp_ev, 1)

            act.wait_ge(pads_ready, 2)
            stepped(act, step1, -1, lo1, hi1, NG + 1)

            act.wait_ge(lT_ready, 1)
            act.wait_ge(mlp_ev, 11)
            act.dma_start(mixb_d, mixb_sb[:, :]).then_inc(mix_out, 16)
            act.dma_start(mix_d, mix_sb[:, :, :]).then_inc(mix_out, 16)

            def step2(s, j):
                a = s
                if live(a, NT):
                    wait(act, sum_ready, a + 1)
                    wait(act, result_out[j], (a - j) * (16 // U))
                    act.activation(ring_b[:, j, :], ring_a[:, j % 2, :], ACT.Relu, scale=0.5).then_inc(result_ready, 1)
                    wait(act, result_ready, a + 1)
                    act.dma_start(result_d[bass.ds(a * P, P), :], ring_b[:, j, :]).then_inc(result_out[j], 16)

            step2(0, 0)
            act.wait_ge(mixbd_zero, 1)
            act.wait_ge(mix_out, 32)
            act.wait_ge(mixb_one, 1)
            act.dma_start(mixb_row[0:1, :], mixb_d.rearrange("(a n) c -> a (n c)", a=1)).then_inc(mix_in, 16)
            for s in range(SUB):
                rows = slice(s * C, (s + 1) * C)
                act.dma_start(mix_bd[rows, :, rows],
                              mix_d.rearrange("(g s) i o -> s i g o", s=SUB)[s]).then_inc(mix_in, 16)
            stepped(act, step2, 1, lo2, hi2, NT)

            def step3(g, j):
                if live(g, NG):
                    wait(act, terms_done, g + 1)
                    wait(act, low_done, g - 1)
                    act.copy(terms_t[:, j % 2, :], ps_terms[j % 2][0:RK, 0:P]).then_inc(thigh_ready, 1)
                a = g + 1
                if live(a, NG):
                    ja = (j + 1) % 2
                    wait(act, mixed_done, a + 1)
                    wait(act, lin_done, a - 1)
                    act.copy(high[:, ja, :], ps_mix[ja][:, :]).then_inc(high_ready, 1)
                a = g + 2
                if live(a, NG):
                    ja = (j + 2) % 2
                    wait(act, y_ready, a + 1)
                    wait(act, terms_done, a - 1)
                    act.activation(ysum_cols[:, ja, :], is_sum[:, :], ACT.Copy, scale=ysum[:, ja:ja + 1]).then_inc(ysum_ready, 1)
                a = g + 6
                if live(a, NG):
                    ja = (j + 6) % U
                    wait(act, gathered[ja], (a - ja) * (32 // U))
                    act.copy(gidx[:, ja, :], place_i[:, bass.ds(a, 1), :].rearrange("p a k -> p (a k)")).then_inc(gidx_ready, 1)

            act.wait_ge(place_ready, 1)
            stepped(act, step3, -6, lo3, hi3 - U, NG)

        @block.vector
        def _(dve):
            def transpose_x(a, ja):
                wait(dve, x_in[ja], ring_count(a, ja, XR))
                wait(dve, ph_done, a - 1)
                dve.transpose(ring_a[:, ja % 2, :].rearrange("m (h q i) -> m q h i", h=MH, q=PH),
                              xt[:, ja, :].rearrange("c (h l q) -> c q h l", h=MH, q=PH)).then_inc(xT_ready, 1)

            dve.memset(wfull[:, :, :], 0.0).then_inc(wfull_zero, 1)
            dve.wait_ge(condT_done, 2)
            dve.tensor_copy(condT[:, :], ps_misc[:, 0:N]).then_inc(condT_ready, 1)
            dve.tensor_copy(cwT[:, :], ps_misc[:, N:N + C]).then_inc(condT_ready, 1)
            dve.wait_ge(ctx_mm, 1)
            dve.wait_ge(fs_in, 16)
            dve.tensor_tensor(ctx_sb[:, :], ps_misc[:, 0:C], fs_bc[:, :], ALU.add).then_inc(ctx_ready, 1)
            dve.wait_ge(convw_in, 16 * (C // CG))
            pick_taps(dve.tensor_copy, range(PH // 2), dve_taps)
            transpose_x(0, 0)
            for t in range(SHIFTS):
                dve.wait_ge(wT_done, t + 1)
                dve.tensor_copy(wconv[:, t, :, :].rearrange("k p o -> k (p o)"), ps_w[t][:, 0:P]).then_inc(wconv_ready, 1)

            deqs = [0]

            def deq_step(ins):
                deqs[0] += 1
                ins.then_inc(deq, 1)
                dve.wait_ge(deq, deqs[0])

            def odd_even():
                deq_step(dve.tensor_scalar(odd_i[:, :], lane_i[:, :], 1, None, ALU.bitwise_and))
                deq_step(dve.tensor_copy(odd[:, :], odd_i[:, :]))
                deq_step(dve.tensor_scalar(even[:, :], odd[:, :], -1.0, 1.0, ALU.mult, ALU.add))

            def pick_halves():
                half = orow[:, 1, :].bitcast(I32)
                odd_part = orow[:, 0, :]
                dve.wait_ge(q_in, 16 * 5)
                deq_step(dve.tensor_scalar(half, words[:, :], 16, None, ALU.logical_shift_right))
                deq_step(dve.tensor_scalar(odd_part, half, odd[:, 0:1], None, ALU.mult))
                deq_step(dve.tensor_scalar(half, words[:, :], 65535, None, ALU.bitwise_and))
                deq_step(dve.scalar_tensor_tensor(words[:, :], half, even[:, 0:1], odd_part, ALU.mult, ALU.add))

            def nibbles(first):
                nibble = orow[:, 1, :].bitcast(I32)
                for j in (first, first + 1):
                    deq_step(dve.tensor_scalar(nibble, words[:, :], 4 * j, 15, ALU.logical_shift_right, ALU.bitwise_and))
                    deq_step(dve.tensor_copy(wq[:, j, :], nibble))

            def rank_masks():
                deq_step(dve.tensor_scalar(is_sum[:, :], cls[:, :], 0.0, None, ALU.is_equal))
                deq_step(dve.tensor_scalar(sel_b[:, :], cls[0:2, :], lane[0:2, 0:1], 1.0, ALU.subtract, ALU.is_equal))
                deq_step(dve.tensor_scalar(ones_r[:, :], cls[:, 0:RK], 0.0, 1.0, ALU.mult, ALU.add))
                deq_step(dve.tensor_scalar(cls_i[:, :], lane_i[:, :], B - 1, None, ALU.bitwise_and))
                deq_step(dve.tensor_scalar(cls_i[:, :], cls_i[:, :], 1, None, ALU.logical_shift_right))
                deq_step(dve.tensor_copy(cls_p[:, :], cls_i[:, :]))
                deq_step(dve.tensor_scalar(term[:, 0:1], cls_p[:, :], 0.0, -1.0, ALU.is_equal, ALU.mult))
                for k in range(1, 3):
                    deq_step(dve.tensor_scalar(term[:, k:k + 1], cls_p[:, :], float(k), None, ALU.is_equal))

            full = words[0:RK, :].bitcast(F32)
            full_high = orow[0:RK, 1, :]
            full_low = orow[0:RK, 0, :]

            def rank_sums():
                dve.wait_ge(colsum_done, 1)
                deq_step(dve.tensor_tensor(full, ps_low[0][0:RK, :], scale_bc[0:RK, :], ALU.mult))
                deq_step(dve.scalar_tensor_tensor(full, zero_bc[0:RK, :], float(-L), full, ALU.mult, ALU.add))
                deq_step(dve.tensor_scalar(full, full, term[0:RK, 1:2], None, ALU.mult))

            def rank_rows():
                deq_step(dve.scalar_tensor_tensor(full, zero_bc[0:RK, :], term[0:RK, 0:1], full, ALU.mult, ALU.add))
                deq_step(dve.scalar_tensor_tensor(full, bias_bc[0:RK, :], term[0:RK, 2:3], full, ALU.mult, ALU.add))
                deq_step(dve.tensor_copy(full_high.bitcast(F32R), full))

            def rank_split():
                deq_step(dve.tensor_tensor(full_low, full, full_high, ALU.subtract))
                deq_step(dve.tensor_scalar(full, full_high, even[0:RK, 0:1], None, ALU.mult))
                deq_step(dve.scalar_tensor_tensor(terms_w[:, :], full_low, odd[0:RK, 0:1], full, ALU.mult, ALU.add))

            transpose_x(1, 1)
            dve.wait_ge(consts, N_CONSTS)
            dve.wait_ge(bg_in, 16)

            def mix_softmax(step):
                if step == 3:
                    dve.wait_ge(mlp_mm, 3)
                    dve.tensor_tensor(att_n[:, :], ps_misc[:, 0:E], b2_bc[:, :], ALU.add).then_inc(mlp_ev, 1)
                    dve.wait_ge(mlp_ev, 3)
                    dve.tensor_reduce(att_m[:, :], att_n[:, :], AX.X, ALU.max).then_inc(mlp_ev, 1)
                    dve.wait_ge(mlp_ev, 4)
                    dve.tensor_scalar(att[:, :], att_n[:, :], att_m[:, 0:1], None, ALU.subtract).then_inc(mlp_ev, 1)
                if step == 4:
                    dve.wait_ge(mlp_ev, 6)
                    dve.reciprocal(att_r[:, :], att_s[:, :]).then_inc(mlp_ev, 1)
                    dve.wait_ge(mlp_ev, 7)
                    dve.tensor_scalar(att_n[:, :], att_x[:, :], att_r[:, 0:1], None, ALU.mult).then_inc(mlp_ev, 1)
                if step == 5:
                    dve.wait_ge(mlp_mm, 4)
                    dve.tensor_copy(attT[:, :], ps_misc[0:E, 0:N]).then_inc(mlp_ev, 1)

            def step1(g, j):
                a, b = g - 1, g - 2
                ja, jb = (j - 1) % U, (j - 2) % U
                if isinstance(g, int) and g in (0, 2):
                    dve.wait_ge(ctx_in[g // 2], 16)
                if isinstance(g, int) and g >= hi1:
                    mix_softmax(g - hi1)
                if live(g, NG):
                    wait(dve, conv_done, g + 1)
                    wait(dve, tok_done, g - 1)
                    dve.tensor_tensor(hT[:, j % 2, :].rearrange("m (p s o) -> m s p o", p=PH, s=SUB),
                                      ps_conv[j % 2][:, :].rearrange("m (s p o) -> m s p o", s=SUB, p=PH),
                                      ctx_bc[:, bass.ds(g * P, P)].rearrange("m (s a o) -> m s a o", s=SUB, a=1).to_broadcast((P, SUB, PH, C)),
                                      ALU.add).then_inc(hT_ready, 1)
                if live(g + 2, NG):
                    transpose_x(g + 2, (j + 2) % U)
                if live(a, NG):
                    wait(dve, gate_done, a + 1)
                    dve.tensor_tensor(logit[:, :], ps_gate[:, 0:E], bg_bc[:, :], ALU.add).then_inc(logit_ready, 1)
                if live(b, NG):
                    wait(dve, rank_done, b + 1)
                    wait(dve, base_ready, b)
                    dve.tensor_tensor(rank[:, :], ps_rank[:, 0:E], base[:, :], ALU.add).then_inc(rank_ready, 1)
                if live(a, NG):
                    wait(dve, logit_ready, a + 1)
                if live(b, NG):
                    wait(dve, rank_ready, b + 1)
                    dve.tensor_tensor(base[:, :], base[:, :], ps_rank[:, E:2 * E], ALU.add).then_inc(base_ready, 1)
                if live(a, NG):
                    dve.max(top[:, :], logit[:, :]).then_inc(top_ready, 1)
                    wait(dve, top_ready, a + 1)
                if live(b, NG):
                    for k in range(2):
                        dve.scalar_tensor_tensor(picked[:, k, :], iota_e[:, :], expert_of[:, bass.ds(b, 1), k:k + 1].rearrange("p a k -> p (a k)"),
                                                 rank[:, :], ALU.is_equal, ALU.mult,
                                                 accum_out=row_of[:, bass.ds(b, 1), k:k + 1].rearrange("p a k -> p (a k)")).then_inc(row_ready, 1)
                if live(a, NG):
                    dve.max_index(topi[:, :], top[:, :], logit[:, :]).then_inc(topi_ready, 1)
                if live(b, NG):
                    wait(dve, row_ready, 2 * b + 2)
                    wait(dve, scattered[jb], (b - jb) * (32 // U))
                    dve.tensor_scalar(row_i[:, jb, :], row_of[:, bass.ds(b, 1), :].rearrange("p a k -> p (a k)"), 0.0, None, ALU.add).then_inc(rowi_ready, 1)
                if live(a, NG):
                    wait(dve, topi_ready, a + 1)
                    dve.tensor_scalar(expert_of[:, bass.ds(a, 1), :].rearrange("p a k -> p (a k)"), topi[:, 0:2], 0.0, None, ALU.add).then_inc(expert_ready, 1)
                    wait(dve, expert_ready, a + 1)
                    e1, e2 = (expert_of[:, bass.ds(a, 1), k:k + 1].rearrange("p a k -> p (a k)") for k in range(2))
                    dve.tensor_scalar(chosen1[:, :], iota_e[:, :], e1, None, ALU.is_equal).then_inc(chosen1_ready, 1)
                    wait(dve, chosen1_ready, a + 1)
                    wait(dve, rank_done, a - 3)
                    dve.scalar_tensor_tensor(chosen[:, ja, :], iota_e[:, :], e2, chosen1[:, :], ALU.is_equal, ALU.add).then_inc(chosen_ready, 1)

            stepped(dve, step1, 0, lo1, hi1, NG + 2)

            n = [0]

            def then(*stage):
                for ins in stage:
                    ins.then_inc(table, 1)
                n[0] += len(stage)
                dve.wait_ge(table, n[0])

            dve.wait_ge(base_ready, NG)
            then(dve.scalar_tensor_tensor(tint[:, :], base[:, :], float(P - 1), region[:, :], ALU.add, ALU.subtract))
            then(dve.tensor_scalar(tshift[:, :], tint[:, :], 7, None, ALU.logical_shift_right))
            then(dve.tensor_copy(prefix[:, 0, E:], tshift[:, :]))
            for k in range(3):
                then(dve.tensor_tensor(prefix[:, k + 1, E:], prefix[:, k, E:], prefix[:, k, E - (1 << k):2 * E - (1 << k)], ALU.add))
            then(dve.tensor_tensor(tstart[:, :], prefix[:, 3, E:], prefix[:, 0, E:], ALU.subtract),
                 dve.scalar_tensor_tensor(offs[:, :], prefix[:, 3, E:], float(-P), base[:, :], ALU.mult, ALU.add),
                 dve.tensor_scalar(used[:, :], prefix[:, 3, 2 * E - 1:2 * E], lane[:, 0:1], None, ALU.is_gt))
            then(dve.tensor_copy(doffs[:, 0:1], offs[:, 0:1]),
                 dve.tensor_tensor(doffs[:, 1:E], offs[:, 1:E], offs[:, 0:E - 1], ALU.subtract),
                 dve.tensor_copy(tab_f[:, 2:3], used[:, :]),
                 dve.tensor_scalar(mask[:, :], tstart[:, :], lane[:, 0:1], None, ALU.is_le))
            then(dve.tensor_tensor(mprod[:, :], mask[:, :], doffs[:, :], ALU.mult),
                 dve.tensor_reduce(tsum[:, 1:2], mask[:, :], AX.X, ALU.add))
            then(dve.tensor_reduce(tsum[:, 0:1], mprod[:, :], AX.X, ALU.add),
                 dve.tensor_scalar(tsum[:, 3:4], tsum[:, 1:2], -1.0, None, ALU.add))
            then(dve.scalar_tensor_tensor(tsum[:, 2:3], lane[:, :], float(P), tsum[:, 0:1], ALU.mult, ALU.add))
            then(dve.tensor_scalar(tab_f[:, 0:2], tsum[:, 2:4], used[:, 0:1], None, ALU.mult))
            dve.sem_inc(tab_ready, 1)
            dve.wait_ge(tab_done, 1)
            dve.tensor_copy(tab[:, :], ps_misc[0:3, 256:256 + P]).then_inc(tab_ready, 1)

            for k in range(2):
                dve.wait_ge(mlp_mm, 5 + k)
                src = ps_kernels[k][:, :].rearrange("n (o i) -> n i o", i=C)
                ins = dve.tensor_copy(mix_sb[:, :, k * 16:k * 16 + 16], src)
                if k == 0:
                    ins.then_inc(mlp_ev, 1)
                    dve.wait_ge(mlp_mm, 7)
                    dve.tensor_copy(mixb_sb[:, :], ps_misc[:, 0:C])
                else:
                    ins.then_inc(mlp_ev, 1)

            def find_places(first, last):
                rows2 = row_of[:, :, :].rearrange("p g k -> p (g k)")
                expert2 = expert_of[:, :, :].rearrange("p g k -> p (g k)")
                for e in range(first, last):
                    if e == 0:
                        then(dve.tensor_scalar(shift_s[:, :], expert2, 0.0, offs[:, 0:1], ALU.is_equal, ALU.mult))
                    else:
                        then(dve.tensor_scalar(shift_e[:, :], expert2, float(e), offs[:, e:e + 1], ALU.is_equal, ALU.mult))
                        then(dve.tensor_tensor(shift_s[:, :], shift_s[:, :], shift_e[:, :], ALU.add))
                if last == E:
                    dve.tensor_tensor(place_i[:, :, :].rearrange("p g k -> p (g k)"), rows2, shift_s[:, :], ALU.subtract).then_inc(place_ready, 1)

            dve.wait_ge(be_in, 16)
            dve.wait_ge(head_out, 16 * E)
            dve.wait_ge(tab_ready, 2)

            def step2(s, j):
                a = s + 1
                if live(a, NT):
                    ja = (j + 1) % U
                    wait(dve, list_in[ja], (a - ja) * (64 // U) + 64)
                    wait(dve, exp_done, a - 1)
                    dve.transpose(hT[:, ja % 2, :].rearrange("m (p h r) -> m h p r", p=PH, h=MH),
                                  htok[:, ja, :].rearrange("r (h p l) -> r h p l", h=MH, p=PH)).then_inc(lT_ready, 1)
                if isinstance(s, int) and s in side_work:
                    side_work[s]()
                if live(s, NT):
                    expert = dve.value_load(tab[1:2, bass.ds(s, 1)], min_val=0, max_val=E - 1)
                    wait(dve, exp_done, s + 1)
                    wait(dve, result_ready, s - 1)
                    dve.tensor_tensor(ring_a[:, j % 2, :], ps_exp[j % 2][:, :],
                                      be_bc[:, bass.ds(expert, 1), :].rearrange("p a n -> p (a n)"), ALU.add).then_inc(sum_ready, 1)

            side_work = {1: rank_masks, 2: odd_even, 3: pick_halves, 4: lambda: nibbles(0), 5: lambda: nibbles(2),
                         7: rank_sums, hi2: rank_rows, hi2 + 1: rank_split, hi2 + 2: lambda: find_places(0, 3),
                         hi2 + 3: lambda: find_places(3, 6), hi2 + 4: lambda: find_places(6, E)}

            stepped(dve, step2, -1, lo2, hi2, NT)
            assert deqs[0] == N_DEQ
            dve.wait_ge(mix_in, 16 * (1 + SUB))

            def step3(g, j):
                a, b, c = g + 2, g + 1, g - 1
                ja, jb, jc = (j + 2) % U, (j + 1) % U, (j - 1) % U
                if live(c, NG):
                    wait(dve, lin_done, c + 1)
                    wait(dve, out_ready, c - 3)
                    dve.tensor_tensor(part[:, jc, :], ps_lin[jc % 2][:, :], scale_bc[:, :], ALU.mult).then_inc(scaled_ready, 1)
                if live(a, NG):
                    wait(dve, x3_in[ja], ring_count(a, ja, XR))
                    wait(dve, gathered[ja], (a - ja) * (32 // U) + 32)
                    wait(dve, out_ready, a - 3)
                    dve.tensor_tensor(y_t[:, ja, :], xt[:, ja, :], found[:, ja, 0, :], ALU.add).then_inc(ya_ready, 1)
                if live(c, NG):
                    wait(dve, scaled_ready, c + 1)
                    wait(dve, low_done, c + 1)
                    dve.tensor_tensor(part[:, jc, :], part[:, jc, :], ps_low[jc % 2][:, :], ALU.add).then_inc(part_ready, 1)
                if live(g, NG):
                    wait(dve, thigh_ready, g + 1)
                    lows = terms_t[B:RK, j % 2, :]
                    dve.tensor_tensor(lows, ps_terms[j % 2][B:RK, 0:P], lows.bitcast(F32), ALU.subtract).then_inc(tlow_ready, 1)
                if live(b, NG):
                    wait(dve, high_ready, b + 1)
                    wait(dve, lin_done, b - 1)
                    dve.tensor_tensor(low[:, jb % 2, :], ps_mix[jb % 2][:, :], high[:, jb % 2, :].bitcast(F32), ALU.subtract).then_inc(low_ready, 1)
                if live(a, NG):
                    wait(dve, ya_ready, a + 1)
                    wait(dve, ysum_ready, a - 1)
                    dve.scalar_tensor_tensor(y_t[:, ja, :], y_t[:, ja, :], 1.0, found[:, ja, 1, :], ALU.mult, ALU.add,
                                             accum_out=ysum[:, ja % 2:ja % 2 + 1]).then_inc(y_ready, 1)

            stepped(dve, step3, -2, lo3, hi3, NG + 1)

        @block.tensor
        def _(pe):
            def warm_up(times):
                for _ in range(times):
                    pe.transpose(bank[0][:, 0:P], ident[:, :], ident[:, :])

            def transpose_phases(a, ja):
                wait(pe, xT_ready, a + 1)
                wait(pe, ph_ready, a)
                for h in range(MH):
                    mm = pe.transpose(ps_ph[:, h * P:(h + 1) * P], ring_a[:, ja % 2, h * P:(h + 1) * P], ident[:, :])
                mm.then_inc(ph_done, 1)

            pe.wait_ge(ident_ready, 2)
            pe.wait_ge(cond_in, 32)
            pe.transpose(ps_misc[:, 0:N], cond_sb[:, :], ident[:, :]).then_inc(condT_done, 1)
            pe.transpose(ps_misc[:, N:N + C], cw_sb[:, :], ident[0:C, 0:C]).then_inc(condT_done, 1)
            pe.wait_ge(condT_ready, 2)
            pe.matmul(ps_misc[:, 0:C], condT[:, :], cwT[:, :], start=True, stop=True).then_inc(ctx_mm, 1)
            warm_up(WARM_START)
            for t in range(SHIFTS):
                pe.wait_ge(dve_taps, t + 1)
                pe.wait_ge(act_taps, t + 1)
                for p in range(PH):
                    mm = pe.transpose(ps_w[t][:, p * C:(p + 1) * C],
                                      wsel[:, t * PH + p, :, :].rearrange("o q i -> o (q i)"), ident[0:C, 0:C])
                mm.then_inc(wT_done, 1)
            transpose_phases(0, 0)
            warm_up(WARM_START)

            def mix_layers(step):
                if step == 0:
                    pe.wait_ge(mlp_in, 16 * 8)
                    pe.matmul(ps_misc[:, 0:N], w0_sb[:, :], condT[:, :], start=True, stop=True).then_inc(mlp_mm, 1)
                if step == 1:
                    pe.wait_ge(mlp_ev, 1)
                    pe.matmul(ps_misc[:, 0:N], w1_sb[:, :], g0[:, :], start=True, stop=True).then_inc(mlp_mm, 1)
                if step == 2:
                    pe.wait_ge(mlp_ev, 2)
                    pe.matmul(ps_misc[:, 0:E], g1[:, :], w2_sb[:, :], start=True, stop=True).then_inc(mlp_mm, 1)
                if step == 4:
                    pe.wait_ge(mlp_ev, 8)
                    pe.transpose(ps_misc[0:E, 0:N], att_n[:, :], ident[:, :]).then_inc(mlp_mm, 1)
                if step == NG + 1 - hi1:
                    pe.wait_ge(mlp_ev, 9)
                    for k in range(2):
                        pe.matmul(ps_kernels[k][:, :], attT[:, :], mixw_sb[:, k * 512:(k + 1) * 512], start=True, stop=True).then_inc(mlp_mm, 1)
                    pe.matmul(ps_misc[:, 0:C], attT[:, :], mixb_w[:, :], start=True, stop=True).then_inc(mlp_mm, 1)

            def count_ranks(a, ja):
                wait(pe, chosen_ready, a + 1)
                wait(pe, base_ready, a)
                pe.matmul(ps_rank[:, 0:E], before[:, :], chosen[:, ja, :], start=True, stop=True)
                pe.matmul(ps_rank[:, E:2 * E], ones[:, :], chosen[:, ja, :], start=True, stop=True).then_inc(rank_done, 1)

            def gate_and_rows(a, ja):
                wait(pe, hT_ready, a + 1)
                wait(pe, logit_ready, a)
                if isinstance(a, int) and a == 0:
                    pe.wait_ge(gate_in, 16)
                    pe.wait_ge(consts, N_CONSTS)
                for p in range(PH):
                    mm = pe.matmul(ps_gate[:, 0:P], hT[:, ja % 2, p * P:(p + 1) * P], wg[:, p, :],
                                   start=(p == 0), stop=(p == PH - 1))
                mm.then_inc(gate_done, 1)
                wait(pe, tok_ready, a)
                for p in range(PH):
                    mm = pe.transpose(ps_tok[:, p * P:(p + 1) * P], hT[:, ja % 2, p * P:(p + 1) * P], ident[:, :])
                mm.then_inc(tok_done, 1)

            def step1(g, j):
                if live(g, NG):
                    wait(pe, ph_ready, g + 1)
                    wait(pe, hT_ready, g - 1)
                    if isinstance(g, int) and g == 0:
                        pe.wait_ge(wconv_ready, SHIFTS)
                    for s in range(SUB):
                        for t in range(SHIFTS):
                            mm = pe.matmul(ps_conv[j % 2][:, s * P:(s + 1) * P], phases[:, j % 2, s, t:t + P],
                                           wconv[:, t, :, :].rearrange("k p o -> k (p o)"),
                                           start=(t == 0), stop=(t == SHIFTS - 1))
                    mm.then_inc(conv_done, 1)
                if live(g + 1, NG):
                    transpose_phases(g + 1, j + 1)
                for_rank = (count_ranks, g - 2, (j - 2) % U)
                for_gate = (gate_and_rows, g - 1, (j - 1) % U)
                last = isinstance(g, int) and g == NG
                for part, a, ja in (for_gate, for_rank) if last else (for_rank, for_gate):
                    if live(a, NG):
                        part(a, ja)
                if isinstance(g, int) and g >= hi1:
                    mix_layers(g - hi1)

            stepped(pe, step1, 0, lo1, hi1, NG + 2)

            pe.wait_ge(tab_ready, 1)
            pe.transpose(ps_misc[0:3, 256:256 + P], tab_f[:, :], ident[:, :]).then_inc(tab_done, 1)
            for _ in range(WARM):
                pe.transpose(bank[6][:, 0:P], ident[:, :], ident[:, :])
            pe.wait_ge(tab_ready, 2)
            pe.wait_ge(we_in, 16 * E)

            def product(s, j):
                expert = pe.value_load(tab[1:2, bass.ds(s, 1)], min_val=0, max_val=E - 1)
                wait(pe, lT_ready, s + 1)
                wait(pe, sum_ready, s - 1)
                for p in range(PH):
                    mm = pe.matmul(ps_exp[j % 2][:, :], hT[:, j % 2, p * P:(p + 1) * P],
                                   we[:, bass.ds(expert, 1), p, :].rearrange("m a n -> m (a n)"),
                                   start=(p == 0), stop=(p == PH - 1))
                mm.then_inc(exp_done, 1)

            def step2(s, j):
                if isinstance(s, int) and s >= SURE:
                    in_use = pe.value_load(tab[2:3, s:s + 1], min_val=0, max_val=1)
                    with pe.If(in_use > 0):
                        product(s, j)
                    with pe.Else():
                        pe.wait_ge(exp_done, s)
                        pe.wait_ge(lT_ready, s + 1)
                        pe.sem_inc(exp_done, 1)
                else:
                    product(s, j)
                if isinstance(s, int) and s == 6:
                    pe.wait_ge(deq, N_NIBBLES + 9)
                    for q in range(4):
                        mm = pe.matmul(ps_low[0][0:RK, :], ones_r[:, :], wq[:, q, :], start=(q == 0), stop=(q == 3))
                    mm.then_inc(colsum_done, 1)

            stepped(pe, step2, 0, lo2, hi2, NT)
            pe.wait_ge(mix_in, 16 * (1 + SUB))
            pe.wait_ge(deq, N_DEQ)
            for _ in range(WARM_END):
                pe.matmul(bank[6][:, :], wq[:, 0, 0:P], wq[:, 0, :], start=True, stop=True)

            def step3(g, j):
                a = g + 1
                if live(a, NG):
                    ja = (j + 1) % U
                    wait(pe, y_ready, a + 1)
                    wait(pe, low_ready, a - 1)
                    for q in range(4):
                        mm = pe.matmul(ps_mix[ja % 2][:, q * P:(q + 1) * P], y_t[:, ja, q:L:4],
                                       mix_bd[:, bass.ds(a, 1), :].rearrange("c a t -> c (a t)"), start=True, stop=True)
                    mm.then_inc(mixed_done, 1)
                if live(g, NG):
                    wait(pe, low_ready, g + 1)
                    wait(pe, scaled_ready, g - 1)
                    for h, half in enumerate((high, low)):
                        for q in range(4):
                            mm = pe.matmul(ps_lin[j % 2][:, :], half[:, j % 2, q * P:(q + 1) * P], wq[:, q, :],
                                           start=(h == q == 0), stop=(h == 1 and q == 3))
                    mm.then_inc(lin_done, 1)
                if live(a, NG):
                    wait(pe, ysum_ready, a + 1)
                    wait(pe, tlow_ready, a - 1)
                    terms = ps_terms[ja % 2][:, 0:P]
                    pe.matmul(terms, ysum_cols[:, ja % 2, :], mix_bd[:, bass.ds(a, 1), :].rearrange("c a t -> c (a t)"), start=True, stop=False)
                    pe.matmul(terms, sel_b[:, :], mixb_row[:, bass.ds(a * P, P)], start=False, stop=True).then_inc(terms_done, 1)
                if live(g, NG):
                    wait(pe, tlow_ready, g + 1)
                    wait(pe, part_ready, g - 1)
                    pe.matmul(ps_low[j % 2][:, :], terms_t[:, j % 2, :], terms_w[:, :], start=True, stop=True).then_inc(low_done, 1)

            stepped(pe, step3, -1, lo3, hi3, NG)


_INS = ['x', 'cond_128', 'fside_S_0', 'L0_cond_weight', 'L0_cond_c_weight', 'L0_ffn_W_gate', 'L0_ffn_b_gate',
        'L0_ffn_W_e', 'L0_ffn_b_e', 'L1_cond_W0', 'L1_cond_b0', 'L1_cond_W1', 'L1_cond_b1', 'L1_cond_W2',
        'L1_cond_b2', 'L1_cond_weight', 'L1_cond_bias_k', 'L1_ffn_qweight', 'L1_ffn_scales', 'L1_ffn_zeros',
        'L1_ffn_bias']


def kernel(**inputs):
    import concourse.bacc as bacc
    from concourse.bass_utils import run_bass_kernel_spmd

    nc = bacc.Bacc("TRN2", target_bir_lowering=False, num_devices=1)
    arrays, args = {}, []
    for name in _INS:
        a = np.ascontiguousarray(inputs[name])
        arrays[f"in_{name}"] = a
        args.append(nc.dram_tensor(f"in_{name}", a.shape, mybir.dt.from_np(a.dtype), kind="ExternalInput").ap())
    result = nc.dram_tensor("out", (N, C, L), F32, kind="ExternalOutput").ap()
    build_program(nc, *args, result)
    r = run_bass_kernel_spmd(nc, [arrays], core_ids=[0])
    return r.results[0]["out"]
```
